# Optimizing a Trainium2 kernel written in Bass

```python
import numpy as np
import jax
import jax.numpy as jnp

def _softmax(x, axis=-1):
    return jax.nn.softmax(x, axis=axis)

def _gelu(x):
    return jax.nn.gelu(x, approximate=True)

def _silu(x):
    return jax.nn.silu(x)

def _sigmoid(x):
    return jax.nn.sigmoid(x)

def _layernorm(x, axis=-1, eps=1e-05):
    m = jnp.mean(x, axis=axis, keepdims=True)
    v = jnp.var(x, axis=axis, keepdims=True)
    return (x - m) / jnp.sqrt(v + eps)

def _scatter_add(tgt, idx, src, axis=0):
    return tgt.at[idx].add(src)

def _segment_sum(src, seg, n):
    return jax.ops.segment_sum(src, seg, n)
kernel_name = 'mk_cond_resid_d2_seqx_r8_b74d69'

def setup_inputs(seed: int=0):
    np.random.seed(seed)
    _w = jnp.asarray

    def _rec_inputs():
        import jax
        import jax.numpy as jnp
        _rk = jax.random.key(seed)
        x = -7.109e-05 + 0.9999 * jax.random.normal(jax.random.fold_in(_rk, 1), (64, 32, 512), jnp.float32)
        _lenS = 32 - jax.random.randint(jax.random.fold_in(_rk, 7), (64,), 0, max(1, 32 // 4) + 1, jnp.int32)
        _lenS2 = 32 - jax.random.randint(jax.random.fold_in(_rk, 8), (64,), 0, max(1, 32 // 4) + 1, jnp.int32)
        itok_B_0_15 = jax.random.randint(jax.random.fold_in(_rk, 11), (64,), 0, 16, jnp.int32)
        itok_B_0_23 = jax.random.randint(jax.random.fold_in(_rk, 12), (64,), 0, 24, jnp.int32)
        return (x, itok_B_0_15, itok_B_0_23)
    x, itok_B_0_15, itok_B_0_23 = _rec_inputs()

    def _L0_cond_setup():
        import jax, jax.numpy as jnp
        import numpy as np
        MAX_LORAS = 16
        IN, OUT = (512, 512)
        B, S = (8, 256)
        key = jax.random.key(seed)
        k1, k2, k3 = jax.random.split(key, 3)
        x = jax.random.normal(k1, (B, S, IN), dtype=jnp.float32)
        adapter_ids = jax.random.randint(k2, (B,), 0, MAX_LORAS)
        weight = jax.random.normal(k3, (MAX_LORAS, OUT, IN), dtype=jnp.float32) * 0.02
        return {'x': x, 'adapter_ids': adapter_ids, 'weight': weight}
    _L0_cond_all = _L0_cond_setup()
    _L0_cond_in = {k: v for k, v in _L0_cond_all.items() if k in ('weight',)}
    del _L0_cond_all

    def _L1_cond_setup():
        import jax, jax.numpy as jnp
        import numpy as np
        R = 16
        ALPHA = 32
        SCALING = ALPHA / R
        SLOTS = 32
        IN_F = 512
        OUT_F = 512
        B, T = (8, 128)
        key = jax.random.key(seed)
        k1, k2, k3, k4, k5, k6 = jax.random.split(key, 6)
        x = jax.random.normal(k1, (B, T, IN_F), dtype=jnp.float32)
        adapter_mapping = jax.random.randint(k2, (B,), 0, SLOTS, dtype=jnp.int32)
        W = jax.random.normal(k3, (OUT_F, IN_F), dtype=jnp.float32) * 0.02
        b = jax.random.normal(k4, (OUT_F,), dtype=jnp.float32) * 0.02
        lora_As = jax.random.normal(k5, (SLOTS, IN_F, R), dtype=jnp.float32) * 0.02
        lora_Bs = jax.random.normal(k6, (SLOTS, R, OUT_F), dtype=jnp.float32) * 0.02
        return {'x': x, 'adapter_mapping': adapter_mapping, 'W': W, 'b': b, 'lora_As': lora_As, 'lora_Bs': lora_Bs}
    _L1_cond_all = _L1_cond_setup()
    _L1_cond_in = {k: v for k, v in _L1_cond_all.items() if k in ('W', 'b', 'lora_As', 'lora_Bs')}
    del _L1_cond_all
    return {'x': x, 'itok_B_0_15': itok_B_0_15, 'itok_B_0_23': itok_B_0_23, 'L0_cond_weight': _L0_cond_in['weight'], 'L1_cond_W': _L1_cond_in['W'], 'L1_cond_b': _L1_cond_in['b'], 'L1_cond_lora_As': _L1_cond_in['lora_As'], 'L1_cond_lora_Bs': _L1_cond_in['lora_Bs']}

def reference(x, itok_B_0_15, itok_B_0_23, L0_cond_weight, L1_cond_W, L1_cond_b, L1_cond_lora_As, L1_cond_lora_Bs):
    import jax
    import jax.numpy as jnp

    def _L0_cond_ref(x, adapter_ids, weight):
        import jax, jax.numpy as jnp
        import numpy as np
        MAX_LORAS = 16
        IN, OUT = (512, 512)
        B, S = (8, 256)
        w = weight[adapter_ids]
        return jnp.einsum('bsi,boi->bso', x, w)

    def _L1_cond_ref(x, adapter_mapping, W, b, lora_As, lora_Bs):
        import jax, jax.numpy as jnp
        import numpy as np
        R = 16
        ALPHA = 32
        SCALING = ALPHA / R
        SLOTS = 32
        IN_F = 512
        OUT_F = 512
        B, T = (8, 128)
        base_out = jnp.einsum('bti,oi->bto', x, W) + b
        A = lora_As[adapter_mapping]
        Bm = lora_Bs[adapter_mapping]
        lora_h = jnp.einsum('bti,bir->btr', x, A)
        lora_out = jnp.einsum('btr,bro->bto', lora_h, Bm)
        return base_out + lora_out * SCALING
    x = x + _L0_cond_ref(x, itok_B_0_15, L0_cond_weight)
    x = x + _L1_cond_ref(x, itok_B_0_23, L1_cond_W, L1_cond_b, L1_cond_lora_As, L1_cond_lora_Bs)
    return x

_drawn_inputs = setup_inputs


def setup_inputs(seed=0):
    import zlib

    import numpy as np

    out = dict(_drawn_inputs(seed))
    spreads = {}
    factors = {'L1_cond_b': 3.658}
    for name, (base, spread) in spreads.items():
        noise = np.random.default_rng([zlib.crc32(name.encode()), seed]).standard_normal(out[name].shape)
        drawn = base * np.exp(spread * noise) if base else spread * noise
        out[name] = jnp.asarray(drawn.astype(out[name].dtype))
    for name, factor in factors.items():
        out[name] = (out[name] * factor).astype(out[name].dtype)
    return out
```

```python
import concourse.bass as bass
from concourse import mybir
from contextlib import ExitStack

B, T, D = 64, 32, 512
NA, SLOTS, R = 16, 32, 16
SCALING = 2.0
P = 128
C = D // P
G = P // T
MAXU = NA + (B - NA) // G
TABU = MAXU + 2
NSLOT = G * TABU
TILES = B // G
PAIRS = TILES // 2
NW = 4
RANKS = B + G

LT, IOTA, K4, B32, P32, P16, ODD, EVEN, ONE, MASK, IDENT = 0, 64, 192, 208, 240, 241, 242, 243, 244, 308, 564
NCONST = IDENT + P
PLAN_ONEHOT, PLAN_ALL = 3, 19
T_ADAPTER, T_RANK, T_COUNT = 0, 32, 64


def two_adapter_layers(nc, x, meta, weights, w1, bias, lora_a, lora_b, consts, out):
    f32, f32r, i32 = mybir.dt.float32, mybir.dt.float32r, mybir.dt.int32
    ALU, ACT, AX = mybir.AluOpType, mybir.ActivationFunctionType, mybir.AxisListType

    ctx = ExitStack()
    with ctx:
        def sb(name, shape, dt=f32):
            return ctx.enter_context(nc.sbuf_tensor(name, shape, dt))

        def bank(name):
            return ctx.enter_context(nc.psum_tensor(name, [P, 512], f32))

        def sem(name):
            return ctx.enter_context(nc.semaphore(name))

        cst = sb("cst", [P, NCONST])
        ident = cst[:, IDENT:IDENT + P]
        mt = sb("mt", [B, 66], i32)
        mf = sb("mf", [B, 66])
        same = sb("same", [B, B])
        within = sb("within", [B, 1])
        onehot = sb("onehot", [B, NA])
        below = sb("below", [B, NA])
        count = sb("count", [B, NA])
        fours = sb("fours", [B, NA, NA])
        units_of = sb("units_of", [B, NA])
        prod = sb("prod", [B, 2, NA])
        before = sb("before", [B, 2])
        n_units = sb("n_units", [B, 1])
        slot_rank = sb("slot_rank", [B, 2])
        rank_m = sb("rank_m", [B, 1])
        place = sb("place", [B, NSLOT + B])
        m16 = sb("m16", [B, 32])
        table = sb("table", [1, 96], i32)
        rows = sb("rows", [P, TABU + TILES], i32)
        odd_part = sb("odd_part", [P, PAIRS])
        even_part = sb("even_part", [P, PAIRS])
        lora_rows = sb("lora_rows", [P, PAIRS], i32)

        w_raw = sb("w_raw", [P, NW, C, D])
        w_hi = sb("w_hi", [P, 2, C, D], f32r)
        w_lo = sb("w_lo", [P, 2, C, D], f32r)
        w1_raw = sb("w1_raw", [P, C, D])
        w1_hi = sb("w1_hi", [P, C, D], f32r)
        w1_lo = sb("w1_lo", [P, C, D], f32r)
        x_tok = sb("x_tok", [P, 4, D])
        xT_hi = sb("xT_hi", [P, 2, D], f32r)
        xT_lo = sb("xT_lo", [P, 2, D], f32r)
        y_tok = sb("y_tok", [P, 2, D])
        x1T = sb("x1T", [P, C, RANKS * T])
        x1_hi = sb("x1_hi", [P, 2, C, 2 * P], f32r)
        x1_lo = sb("x1_lo", [P, 2, C, 2 * P], f32r)
        a_raw = sb("a_raw", [P, 2, D])
        b_raw = sb("b_raw", [P, 2, D])
        a_hi = sb("a_hi", [P, D], f32r)
        a_lo = sb("a_lo", [P, D], f32r)
        b_hi = sb("b_hi", [P, D], f32r)
        b_lo = sb("b_lo", [P, D], f32r)
        h_own = sb("h_own", [P, 2 * P])
        h_hi = sb("h_hi", [P, 2 * P], f32r)
        h_lo = sb("h_lo", [P, 2 * P], f32r)
        bias_sb = sb("bias_sb", [P, D])
        o_tok = sb("o_tok", [P, 4, D])

        Y = [bank("Y0"), bank("Y1")]
        YT = [bank("YT0"), bank("YT1")]
        XT = [bank("XT0"), bank("XT1")]
        Hb = bank("Hb")
        S = bank("S")
        counts_ps = S[0:B, 0:NA]
        table_ps = S[0:1, 32:32 + 96]
        rows_ps = S[:, 128:128 + TABU + TILES]
        lora_ps = Hb[:, 0:2 * PAIRS]

        s_cst, s_meta, s_w1, s_bias = sem("s_cst"), sem("s_meta"), sem("s_w1"), sem("s_bias")
        w_in = [sem(f"w_in{k}") for k in range(NW)]
        x_in = [sem(f"x_in{k}") for k in range(4)]
        a_in = [sem(f"a_in{k}") for k in range(2)]
        b_in = [sem(f"b_in{k}") for k in range(2)]
        o_out = [sem(f"o_out{k}") for k in range(4)]
        s_plan = sem("s_plan")
        counts_ready = sem("counts_ready")
        tables_ps_ready = sem("tables_ps_ready")
        table_ready = sem("table_ready")
        lora_rows_ready = sem("lora_rows_ready")
        x_turned, x_hi_ready, x_lo_ready = sem("x_turned"), sem("x_hi_ready"), sem("x_lo_ready")
        w_hi_ready = sem("w_hi_ready")
        w_loA_ready, w_loB_ready = sem("w_loA_ready"), sem("w_loB_ready")
        mm_done, y_ready, y_turned, x1_ready = sem("mm_done"), sem("y_ready"), sem("y_turned"), sem("x1_ready")
        w1_diag, w1_hi_ready, w1_lo_ready = sem("w1_diag"), sem("w1_hi_ready"), sem("w1_lo_ready")
        x1_hi_ready, x1_lo_ready = sem("x1_hi_ready"), sem("x1_lo_ready")
        a_turned, a_hi_ready, a_lo_ready = sem("a_turned"), sem("a_hi_ready"), sem("a_lo_ready")
        b_hi_ready, b_lo_ready = sem("b_hi_ready"), sem("b_lo_ready")
        h_done, h_own_ready, h_hi_ready, h_lo_ready = sem("h_done"), sem("h_own_ready"), sem("h_hi_ready"), sem("h_lo_ready")
        tile_done, o_free = sem("tile_done"), sem("o_free")
        o_ready = [sem("o_ready0"), sem("o_ready1")]

        row_at = sb("row_at", [P, 4], i32)
        row_copied, row_seen = sem("row_copied"), sem("row_seen")
        block = ctx.enter_context(nc.Block())

        def all_units(eng, unit):
            n = eng.value_load(table[0:1, T_COUNT:T_COUNT + 1], min_val=NA, max_val=MAXU)
            ran = eng.alloc_register(f"ran_{eng.engine.name}")
            last_k = eng.alloc_register(f"last_k_{eng.engine.name}")
            unit(0, 0)
            unit(1, 1)
            with eng.Fori(2, n, 4) as v:
                unit(v, 2)
                unit(v + 1, 3)
                eng.reg_mov(ran, v + 2)
                eng.reg_mov(last_k, 2)
                with eng.If(v + 2 < n):
                    unit(v + 2, 0)
                    unit(v + 3, 1)
                    eng.reg_mov(ran, v + 4)
                    eng.reg_mov(last_k, 0)
            return eng.snap(ran, min_val=NA, max_val=MAXU), eng.snap(last_k, min_val=0, max_val=2)

        def all_pairs(eng, pair):
            with eng.Fori(0, PAIRS // 2 - 1) as half:
                g = 2 * half
                pair(g, 0, False)
                pair(g + 1, 1, False)
            pair(PAIRS - 2, 0, False)
            pair(PAIRS - 1, 1, True)

        @block.sync
        def _(sp):
            sp.dma_start(mt[:, :], meta).then_inc(s_meta, 16)
            sp.dma_start(cst[:, :], consts).then_inc(s_cst, 16)
            sp.dma_start(w1_raw[:, :, :], w1).then_inc(s_w1, 16)
            sp.dma_start(bias_sb[:, :], bias).then_inc(s_bias, 16)
            sp.wait_ge(table_ready, 4)

            def adapter_in(u, k):
                a = sp.value_load(table[0:1, bass.ds(T_ADAPTER + u, 1)], min_val=0, max_val=NA - 1)
                if not isinstance(u, int):
                    sp.wait_ge(w_loA_ready, u - 3)
                    sp.wait_ge(w_loB_ready, u - 3)
                sp.dma_start(w_raw[:, k, :, :], weights[bass.ds(a, 1), :, :, :]).then_inc(w_in[k], 16)

            n = sp.value_load(table[0:1, T_COUNT:T_COUNT + 1], min_val=NA, max_val=MAXU)
            for u in range(4):
                adapter_in(u, u)
            with sp.Fori(4, n, 4) as v:
                adapter_in(v, 0)
                adapter_in(v + 1, 1)
                with sp.If(v + 2 < n):
                    adapter_in(v + 2, 2)
                    adapter_in(v + 3, 3)

        @block.gpsimd
        def _(pool):
            def gather_x(u, k):
                if isinstance(u, int):
                    at = rows[:, u:u + 1]
                else:
                    pool.wait_ge(y_ready, u - 3)
                    pool.tensor_copy(row_at[:, k:k + 1], rows[:, bass.ds(u, 1)]).then_inc(row_copied, 1)
                    pool.wait_ge(row_copied, u - 3)
                    pool.sem_inc(row_seen, 1)
                    at = row_at[:, k:k + 1]
                pool.indirect_dma_start(x_tok[:, k, :], None, x, bass.IndirectOffsetOnAxis(ap=at, axis=0))\
                    .then_inc(x_in[k], 16)

            def gather_lora(g):
                for raw, rows_of, landed in ((a_raw, lora_a, a_in), (b_raw, lora_b, b_in)):
                    pool.indirect_dma_start(raw[:, g % 2, :], None, rows_of,
                                            bass.IndirectOffsetOnAxis(ap=lora_rows[:, g:g + 1], axis=0))\
                        .then_inc(landed[g % 2], 16)

            pool.sem_inc(o_free, 4)
            pool.wait_ge(table_ready, 4)
            for u in range(2):
                gather_x(u, u)
            pool.wait_ge(w1_hi_ready, 1)
            pool.tensor_tensor(w1_lo[:, :, :], w1_raw[:, :, :], w1_hi[:, :, :], ALU.subtract).then_inc(w1_lo_ready, 1)

            def unit(u, k):
                q = k % 2
                pool.wait_ge(w_hi_ready, 2 * u + 1)
                pool.tensor_tensor(w_lo[:, q, 2:4, :], w_raw[:, k, 2:4, :], w_hi[:, q, 2:4, :], ALU.subtract)\
                    .then_inc(w_loB_ready, 1)
                gather_x(u + 2, (k + 2) % 4)

            n = pool.value_load(table[0:1, T_COUNT:T_COUNT + 1], min_val=NA, max_val=MAXU)
            unit(0, 0)
            unit(1, 1)
            pool.wait_ge(lora_rows_ready, 1)
            for g in range(2):
                gather_lora(g)
            with pool.Fori(2, n, 4) as v:
                unit(v, 2)
                unit(v + 1, 3)
                with pool.If(v + 2 < n):
                    unit(v + 2, 0)
                    unit(v + 3, 1)

            for g in range(PAIRS):
                for s in range(2):
                    t = 2 * g + s
                    pool.wait_ge(o_ready[s], g + 2)
                    pool.indirect_dma_start(out, bass.IndirectOffsetOnAxis(ap=rows[:, TABU + t:TABU + t + 1], axis=0),
                                            o_tok[:, t % 4, :], None).then_inc(o_out[t % 4], 16)
                    if t >= 2:
                        pool.wait_ge(o_out[(t - 2) % 4], 16 * ((t - 2) // 4 + 1))
                        pool.sem_inc(o_free, 1)
                if g + 2 < PAIRS:
                    pool.wait_ge(a_turned, g + 1)
                    pool.wait_ge(b_hi_ready, g + 1)
                    pool.wait_ge(b_lo_ready, g + 1)
                    gather_lora(g + 2)
            for k in range(4):
                pool.wait_ge(o_out[k], 16 * TILES // 4)

        @block.scalar
        def _(act):
            act.sem_inc(x1_ready, 1)
            act.wait_ge(w1_diag, C)
            act.activation(w1_hi[:, :, :], w1_raw[:, :, :], ACT.Copy).then_inc(w1_hi_ready, 1)

            def take_x1(u, k):
                r = act.value_load(table[0:1, bass.ds(T_RANK + u, 1)], min_val=0, max_val=B)
                act.wait_ge(y_turned, u + 1)
                act.wait_ge(x1_ready, u + 1)
                act.activation(x1T[:, :, bass.ds(T * r, P)], YT[k % 2][:, :].rearrange("p (c t) -> p c t", c=C),
                               ACT.Copy).then_inc(x1_ready, 1)

            def unit(u, k):
                q = k % 2
                act.wait_ge(w_in[k], 4 * (u - k) + 16)
                if k >= 2 or not isinstance(u, int):
                    act.wait_ge(mm_done, u - 1)
                act.activation(w_hi[:, q, 2:4, :], w_raw[:, k, 2:4, :], ACT.Copy).then_inc(w_hi_ready, 1)
                act.activation(w_hi[:, q, 0:2, :], w_raw[:, k, 0:2, :], ACT.Copy).then_inc(w_hi_ready, 1)
                if not isinstance(u, int):
                    take_x1(u - 2, k)
                act.wait_ge(x_turned, u + 1)
                act.activation(xT_hi[:, q, :], XT[q][:, :], ACT.Copy).then_inc(x_hi_ready, 1)

            act.wait_ge(table_ready, 4)
            n, _ = all_units(act, unit)
            take_x1(n - 2, 0)
            take_x1(n - 1, 1)

            def round_a(g):
                act.wait_ge(a_turned, g + 1)
                act.wait_ge(h_done, g + 1)
                act.activation(a_hi[:, :], S[:, :], ACT.Copy).then_inc(a_hi_ready, 1)

            def round_b(g, k):
                act.wait_ge(b_in[k], 8 * (g - k) + 16)
                act.wait_ge(tile_done, 2 * g + 1)
                act.activation(b_hi[:, :], b_raw[:, k, :], ACT.Copy).then_inc(b_hi_ready, 1)

            act.wait_ge(x1_ready, n + 1)
            act.activation(x1_hi[:, 0, :, :], x1T[:, :, 0:2 * P], ACT.Copy).then_inc(x1_hi_ready, 1)
            round_a(0)
            round_b(0, 0)

            def pair(g, k, last):
                act.wait_ge(h_own_ready, g + 1)
                act.wait_ge(tile_done, 2 * g + 1)
                act.activation(h_hi[:, :], h_own[:, :], ACT.Copy).then_inc(h_hi_ready, 1)
                if not last:
                    act.activation(x1_hi[:, 1 - k, :, :], x1T[:, :, bass.ds(2 * P * (g + 1), 2 * P)], ACT.Copy)\
                        .then_inc(x1_hi_ready, 1)
                    round_a(g + 1)
                    round_b(g + 1, 1 - k)

            all_pairs(act, pair)

        @block.tensor
        def _(pe):
            pe.sem_inc(tile_done, 1)
            pe.sem_inc(h_done, 1)
            pe.wait_ge(s_cst, 16)
            pe.wait_ge(s_plan, PLAN_ONEHOT)
            pe.matmul(counts_ps, cst[0:B, ONE:ONE + B], onehot[:, :], start=True, stop=True).then_inc(counts_ready, 1)
            pe.wait_ge(s_plan, PLAN_ALL)
            pe.matmul(table_ps[:, T_ADAPTER:T_ADAPTER + TABU], mf[:, 64:65], place[:, 0:NSLOT:G], start=True, stop=True)
            pe.matmul(table_ps[:, T_RANK:T_RANK + TABU], rank_m[:, :], place[:, 0:NSLOT:G], start=True, stop=True)
            for j in range(G):
                mm = pe.matmul(rows_ps[T * j:T * j + T, :], cst[0:B, B32:B32 + T], place[:, j:NSLOT + B:G],
                               start=True, stop=True)
            mm.then_inc(tables_ps_ready, 1)
            for j in range(G):
                for e in range(2):
                    mm = pe.matmul(lora_ps[T * j:T * j + T, PAIRS * e:PAIRS * (e + 1)], m16[:, :],
                                   place[:, NSLOT + 2 * j + e:NSLOT + B:8], start=True, stop=True)
            mm.then_inc(tables_ps_ready, 1)

            def turn_x(u, k):
                pe.wait_ge(x_in[k], 4 * (u - k) + 16)
                if k >= 2 or not isinstance(u, int):
                    pe.wait_ge(x_lo_ready, u - 1)
                for c in range(C):
                    mm = pe.transpose(XT[k % 2][:, P * c:P * c + P], x_tok[:, k, P * c:P * c + P], ident)
                mm.then_inc(x_turned, 1)

            def turn_y(u, k):
                q = k % 2
                pe.wait_ge(y_ready, u + 1)
                if k >= 2 or not isinstance(u, int):
                    pe.wait_ge(x1_ready, u)
                for c in range(C):
                    mm = pe.transpose(YT[q][:, P * c:P * c + P], y_tok[:, q, P * c:P * c + P], ident)
                mm.then_inc(y_turned, 1)

            def unit(u, k):
                q = k % 2
                for c in range(C):
                    if c == 0:
                        pe.wait_ge(x_lo_ready, u + 1)
                        pe.wait_ge(w_loA_ready, u + 1)
                    if c == 2:
                        if not (isinstance(u, int) and u == 0):
                            turn_y(u - 1, (k - 1) % 4)
                        turn_x(u + 1, (k + 1) % 4)
                        pe.wait_ge(w_loB_ready, u + 1)
                    xc = slice(P * c, P * c + P)
                    pe.matmul(Y[q][:, :], xT_hi[:, q, xc], w_hi[:, q, c, :], start=(c == 0), stop=False)
                    pe.matmul(Y[q][:, :], xT_hi[:, q, xc], w_lo[:, q, c, :], start=False, stop=False)
                    mm = pe.matmul(Y[q][:, :], xT_lo[:, q, xc], w_hi[:, q, c, :], start=False, stop=(c == C - 1))
                mm.then_inc(mm_done, 1)

            def turn_a(g, k):
                pe.wait_ge(a_in[k], 8 * (g - k) + 16)
                pe.wait_ge(a_lo_ready, g + 1)
                for c in range(C):
                    mm = pe.transpose(S[:, P * c:P * c + P], a_raw[:, k, P * c:P * c + P], ident)
                mm.then_inc(a_turned, 1)

            turn_x(0, 0)
            n, _ = all_units(pe, unit)
            turn_y(n - 1, 1)
            pe.wait_ge(lora_rows_ready, 1)
            turn_a(0, 0)
            pe.wait_ge(w1_lo_ready, 1)

            def pair(g, k, last):
                pe.wait_ge(x1_lo_ready, g + 1)
                pe.wait_ge(a_lo_ready, g + 2)
                for c in range(C):
                    ac = slice(P * c, P * c + P)
                    pe.matmul(Hb[:, 0:2 * P], a_hi[:, ac], x1_hi[:, k, c, :], start=(c == 0), stop=False)
                    pe.matmul(Hb[:, 0:2 * P], a_hi[:, ac], x1_lo[:, k, c, :], start=False, stop=False)
                    mm = pe.matmul(Hb[:, 0:2 * P], a_lo[:, ac], x1_hi[:, k, c, :], start=False, stop=(c == C - 1))
                mm.then_inc(h_done, 1)
                for s in range(2):
                    pe.wait_ge(o_ready[s], g + 1)
                    ts = slice(P * s, P * s + P)
                    for c in range(C):
                        pe.matmul(Y[s][:, :], x1_hi[:, k, c, ts], w1_hi[:, c, :], start=(c == 0), stop=False)
                        pe.matmul(Y[s][:, :], x1_hi[:, k, c, ts], w1_lo[:, c, :], start=False, stop=False)
                        pe.matmul(Y[s][:, :], x1_lo[:, k, c, ts], w1_hi[:, c, :], start=False, stop=False)
                    if s == 0:
                        if not last:
                            turn_a(g + 1, 1 - k)
                        pe.wait_ge(h_lo_ready, g + 2)
                        pe.wait_ge(b_lo_ready, g + 1)
                        pe.wait_ge(b_hi_ready, g + 1)
                    pe.matmul(Y[s][:, :], h_hi[:, ts], b_hi[:, :], start=False, stop=False)
                    pe.matmul(Y[s][:, :], h_hi[:, ts], b_lo[:, :], start=False, stop=False)
                    pe.matmul(Y[s][:, :], h_lo[:, ts], b_hi[:, :], start=False, stop=True).then_inc(tile_done, 1)

            all_pairs(pe, pair)

        @block.vector
        def _(dve):
            steps = [0]

            def step(ins):
                steps[0] += 1
                ins.then_inc(s_plan, 1)
                dve.wait_ge(s_plan, steps[0])

            for credited in (a_lo_ready, h_lo_ready, o_ready[0], o_ready[1]):
                dve.sem_inc(credited, 1)
            iota = cst[0:B, IOTA:IOTA + P]
            dve.wait_ge(s_meta, 16)
            step(dve.tensor_copy(mf[:, :], mt[:, :]))
            dve.wait_ge(s_cst, 16)
            step(dve.scalar_tensor_tensor(same[:, :], mf[:, 0:B], mf[:, 64:65], cst[0:B, LT:LT + B],
                                          ALU.is_equal, ALU.mult))
            step(dve.tensor_scalar(onehot[:, :], iota[:, 0:NA], mf[:, 64:65], None, ALU.is_equal))
            assert steps[0] == PLAN_ONEHOT
            step(dve.tensor_scalar(below[:, :], iota[:, 0:NA], mf[:, 64:65], None, ALU.is_lt))
            step(dve.tensor_reduce(within[:, :], same[:, :], AX.X, ALU.add))
            step(dve.tensor_scalar(m16[:, :], cst[0:B, ONE:ONE + 32], mf[:, 65:66], float(R), ALU.mult, ALU.mult))
            dve.wait_ge(counts_ready, 1)
            step(dve.tensor_copy(count[:, :], counts_ps))
            step(dve.tensor_tensor(fours[:, :, :], count[:, :].unsqueeze(2).to_broadcast([B, NA, NA]),
                                   cst[0:B, K4:K4 + NA].unsqueeze(1).to_broadcast([B, NA, NA]), ALU.is_gt))
            step(dve.tensor_reduce(units_of[:, :], fours[:, :, :], AX.X, ALU.add))
            step(dve.tensor_tensor(prod[:, 0, :], units_of[:, :], below[:, :], ALU.mult))
            step(dve.tensor_tensor(prod[:, 1, :], count[:, :], below[:, :], ALU.mult))
            step(dve.tensor_reduce(before[:, :], prod[:, :, :], AX.X, ALU.add))
            step(dve.tensor_reduce(n_units[:, :], units_of[:, :], AX.X, ALU.add))
            step(dve.scalar_tensor_tensor(slot_rank[:, 0:1], before[:, 0:1], float(G), within[:, :], ALU.mult, ALU.add))
            step(dve.tensor_tensor(slot_rank[:, 1:2], before[:, 1:2], within[:, :], ALU.add))
            step(dve.tensor_scalar(rank_m[:, :], slot_rank[:, 1:2], float(-B), None, ALU.add))
            step(dve.tensor_scalar(place[:, 0:NSLOT], iota[:, 0:NSLOT], slot_rank[:, 0:1], None, ALU.is_equal))
            step(dve.tensor_scalar(place[:, NSLOT:NSLOT + B], iota[:, 0:B], slot_rank[:, 1:2], None, ALU.is_equal))
            step(dve.tensor_copy(table[:, T_COUNT:T_COUNT + 1], n_units[0:1, :]))
            assert steps[0] == PLAN_ALL
            dve.wait_ge(tables_ps_ready, 1)
            dve.tensor_copy(table[:, T_ADAPTER:T_ADAPTER + TABU], table_ps[:, T_ADAPTER:T_ADAPTER + TABU])\
                .then_inc(table_ready, 1)
            dve.tensor_scalar(rows[:, :], rows_ps, cst[:, P32:P32 + 1], None, ALU.add).then_inc(table_ready, 1)
            dve.tensor_scalar(table[:, T_RANK:T_RANK + TABU], table_ps[:, T_RANK:T_RANK + TABU], float(B), None,
                              ALU.add).then_inc(table_ready, 2)
            dve.wait_ge(tables_ps_ready, 2)
            dve.tensor_scalar(odd_part[:, :], lora_ps[:, PAIRS:2 * PAIRS], cst[:, ODD:ODD + 1], cst[:, P16:P16 + 1],
                              ALU.mult, ALU.add).then_inc(s_plan, 1)
            dve.tensor_scalar(even_part[:, :], lora_ps[:, 0:PAIRS], cst[:, EVEN:EVEN + 1], None, ALU.mult)\
                .then_inc(s_plan, 1)
            dve.wait_ge(s_plan, PLAN_ALL + 2)
            dve.tensor_tensor(lora_rows[:, :], even_part[:, :], odd_part[:, :], ALU.add).then_inc(lora_rows_ready, 1)
            dve.wait_ge(s_w1, 16)
            for c in range(C):
                block_c = w1_raw[:, c, P * c:P * c + P]
                dve.tensor_tensor(block_c, block_c, ident, ALU.add).then_inc(w1_diag, 1)

            def add_x(u, q, x_of_u):
                dve.wait_ge(mm_done, u + 1)
                dve.tensor_tensor(y_tok[:, q, :], Y[q][:, :], x_of_u, ALU.add).then_inc(y_ready, 1)

            def unit(u, k):
                q = k % 2
                if not isinstance(u, int):
                    add_x(u - 2, q, x_tok[:, (k - 2) % 4, :])
                dve.wait_ge(w_hi_ready, 2 * u + 2)
                dve.tensor_tensor(w_lo[:, q, 0:2, :], w_raw[:, k, 0:2, :], w_hi[:, q, 0:2, :], ALU.subtract)\
                    .then_inc(w_loA_ready, 1)
                dve.wait_ge(x_hi_ready, u + 1)
                dve.tensor_tensor(xT_lo[:, q, :], XT[q][:, :], xT_hi[:, q, :], ALU.subtract).then_inc(x_lo_ready, 1)

            n, k = all_units(dve, unit)
            x_flat = x_tok[:, :, :].rearrange("p k d -> p (k d)")
            for q in range(2):
                add_x(n - 2 + q, q, x_flat[:, bass.ds(D * (k + q), D)])

            dve.wait_ge(x1_hi_ready, 1)
            dve.tensor_tensor(x1_lo[:, 0, :, :], x1T[:, :, 0:2 * P], x1_hi[:, 0, :, :], ALU.subtract).then_inc(x1_lo_ready, 1)
            dve.wait_ge(a_hi_ready, 1)
            dve.tensor_tensor(a_lo[:, :], S[:, :], a_hi[:, :], ALU.subtract).then_inc(a_lo_ready, 1)
            dve.wait_ge(b_hi_ready, 1)
            dve.tensor_tensor(b_lo[:, :], b_raw[:, 0, :], b_hi[:, :], ALU.subtract).then_inc(b_lo_ready, 1)
            dve.wait_ge(s_bias, 16)

            def pair(g, k, last):
                dve.wait_ge(h_done, g + 2)
                dve.wait_ge(h_lo_ready, g + 1)
                dve.tensor_tensor(h_own[:, :], Hb[:, 0:2 * P], cst[:, MASK:MASK + 2 * P], ALU.mult).then_inc(h_own_ready, 1)
                dve.wait_ge(h_hi_ready, g + 1)
                dve.tensor_tensor(h_lo[:, :], h_own[:, :], h_hi[:, :], ALU.subtract).then_inc(h_lo_ready, 1)
                if not last:
                    dve.wait_ge(x1_hi_ready, g + 2)
                    dve.tensor_tensor(x1_lo[:, 1 - k, :, :], x1T[:, :, bass.ds(2 * P * (g + 1), 2 * P)],
                                      x1_hi[:, 1 - k, :, :], ALU.subtract).then_inc(x1_lo_ready, 1)
                    dve.wait_ge(a_hi_ready, g + 2)
                    dve.tensor_tensor(a_lo[:, :], S[:, :], a_hi[:, :], ALU.subtract).then_inc(a_lo_ready, 1)
                for s in range(2):
                    slot = 2 * k + s
                    dve.wait_ge(tile_done, 2 * g + s + 2)
                    dve.wait_ge(o_free, 2 * g + s + 1)
                    dve.tensor_tensor(o_tok[:, slot, :], Y[s][:, :], bias_sb[:, :], ALU.add).then_inc(o_ready[s], 1)
                if not last:
                    dve.wait_ge(b_hi_ready, g + 2)
                    dve.tensor_tensor(b_lo[:, :], b_raw[:, 1 - k, :], b_hi[:, :], ALU.subtract).then_inc(b_lo_ready, 1)

            all_pairs(dve, pair)


def constants():
    import numpy as np
    p = np.arange(P)
    c = np.zeros((P, NCONST), np.float32)
    b = np.arange(B)
    c[:B, LT:LT + B] = b[None, :] < b[:, None]
    c[:, IOTA:IOTA + P] = p[None, :]
    c[:, K4:K4 + NA] = G * np.arange(NA)
    c[:, B32:B32 + T] = T * p[:, None]
    c[:, P32], c[:, P16] = p % T, p % R
    c[:, ODD], c[:, EVEN] = p // R % 2, 1 - p // R % 2
    c[:, ONE:ONE + B] = 1
    c[:, MASK:MASK + 2 * P] = SCALING * (p[:, None] // R == np.arange(2 * P)[None, :] // T)
    c[:, IDENT:IDENT + P] = np.eye(P)
    return c


def kernel(x, itok_B_0_15, itok_B_0_23, L0_cond_weight, L1_cond_W, L1_cond_b, L1_cond_lora_As, L1_cond_lora_Bs):
    import numpy as np
    import concourse.bacc as bacc
    from concourse.bass_utils import run_bass_kernel_spmd

    ids, ms = np.asarray(itok_B_0_15), np.asarray(itok_B_0_23)
    turned = np.asarray(L0_cond_weight).transpose(0, 2, 1).reshape(NA, C, P, D).transpose(0, 2, 1, 3)
    arrays = {
        "x": np.ascontiguousarray(x).reshape(B * T, D),
        "meta": np.concatenate([np.broadcast_to(ids[None, :], (B, B)), ids[:, None], ms[:, None]], axis=1),
        "weights": turned,
        "w1": np.asarray(L1_cond_W).T.reshape(C, P, D).transpose(1, 0, 2),
        "bias": np.broadcast_to(np.asarray(L1_cond_b)[None, :], (P, D)),
        "lora_a": np.asarray(L1_cond_lora_As).transpose(0, 2, 1).reshape(SLOTS * R, D),
        "lora_b": np.asarray(L1_cond_lora_Bs).reshape(SLOTS * R, D),
        "consts": constants(),
    }
    arrays = {k: np.ascontiguousarray(v) for k, v in arrays.items()}
    nc = bacc.Bacc("TRN2", target_bir_lowering=False, num_devices=1)
    args = [nc.dram_tensor(k, v.shape, mybir.dt.from_np(v.dtype), kind="ExternalInput").ap() for k, v in arrays.items()]
    out = nc.dram_tensor("out", (B * T, D), mybir.dt.float32, kind="ExternalOutput").ap()
    two_adapter_layers(nc, *args, out)
    r = run_bass_kernel_spmd(nc, [arrays], core_ids=[0])
    return r.results[0]["out"].reshape(B, T, D)
```

```python
import concourse.bass as bass
from concourse import mybir
from contextlib import ExitStack

B, T, D = 64, 32, 512
NA, SLOTS, R = 16, 32, 16
SCALING = 2.0
P = 128
C = D // P
G = P // T
MAXU = NA + (B - NA) // G
TABU = MAXU + 3
NSLOT = G * TABU
TILES = B // G
PAIRS = TILES // 2
NW = 4
RANKS = B + G

LT, IOTA, K4, B32, P32, P16, ODD, EVEN, ONE, MASK, IDENT = 0, 64, 192, 208, 240, 241, 242, 243, 244, 308, 564
NCONST = IDENT + P
PLAN_ONEHOT, PLAN_ALL = 2, 20
T_ADAPTER, T_RANK, T_COUNT, T_FIRST = 0, 32, 64, 65


def two_adapter_layers(nc, x, meta, weights, w1, bias, lora_a, lora_b, consts, out):
    f32, f32r, i32 = mybir.dt.float32, mybir.dt.float32r, mybir.dt.int32
    ALU, ACT, AX = mybir.AluOpType, mybir.ActivationFunctionType, mybir.AxisListType

    ctx = ExitStack()
    with ctx:
        def sb(name, shape, dt=f32):
            return ctx.enter_context(nc.sbuf_tensor(name, shape, dt))

        def bank(name):
            return ctx.enter_context(nc.psum_tensor(name, [P, 512], f32))

        def sem(name):
            return ctx.enter_context(nc.semaphore(name))

        cst = sb("cst", [P, NCONST])
        ident = cst[:, IDENT:IDENT + P]
        mt = sb("mt", [B, 66], i32)
        mf = sb("mf", [B, 66])
        same = sb("same", [B, B])
        within = sb("within", [B, 1])
        onehot = sb("onehot", [B, NA])
        below = sb("below", [B, NA])
        count = sb("count", [B, NA])
        fours = sb("fours", [B, NA, NA])
        units_of = sb("units_of", [B, NA])
        prod = sb("prod", [B, 2, NA])
        before = sb("before", [B, 2])
        n_units = sb("n_units", [B, 1])
        first = sb("first", [1, 1])
        slot_rank = sb("slot_rank", [B, 2])
        rank_m = sb("rank_m", [B, 1])
        place = sb("place", [B, NSLOT + B])
        m16 = sb("m16", [B, 32])
        table = sb("table", [1, 96], i32)
        rows = sb("rows", [P, TABU + TILES], i32)
        odd_part = sb("odd_part", [P, PAIRS])
        even_part = sb("even_part", [P, PAIRS])
        lora_rows = sb("lora_rows", [P, PAIRS], i32)

        w_raw = sb("w_raw", [P, NW, C, D])
        w_hi = sb("w_hi", [P, 2, C, D], f32r)
        w_lo = sb("w_lo", [P, 2, C, D], f32r)
        w1_raw = sb("w1_raw", [P, C, D])
        w1_hi = sb("w1_hi", [P, C, D], f32r)
        w1_lo = sb("w1_lo", [P, C, D], f32r)
        x_tok = sb("x_tok", [P, 4, D])
        xT_hi = sb("xT_hi", [P, 2, D], f32r)
        xT_lo = sb("xT_lo", [P, 2, D], f32r)
        y_tok = sb("y_tok", [P, 2, D])
        x1T = sb("x1T", [P, C, RANKS * T])
        x1_hi = sb("x1_hi", [P, 2, C, 2 * P], f32r)
        x1_lo = sb("x1_lo", [P, 2, C, 2 * P], f32r)
        a_raw = sb("a_raw", [P, 2, D])
        b_raw = sb("b_raw", [P, 2, D])
        a_hi = sb("a_hi", [P, D], f32r)
        a_lo = sb("a_lo", [P, D], f32r)
        b_hi = sb("b_hi", [P, D], f32r)
        b_lo = sb("b_lo", [P, D], f32r)
        h_own = sb("h_own", [P, 2 * P])
        h_hi = sb("h_hi", [P, 2 * P], f32r)
        h_lo = sb("h_lo", [P, 2 * P], f32r)
        bias_sb = sb("bias_sb", [P, D])
        o_tok = sb("o_tok", [P, 4, D])

        Y = [bank("Y0"), bank("Y1")]
        YT = [bank("YT0"), bank("YT1")]
        XT = [bank("XT0"), bank("XT1")]
        Hb = bank("Hb")
        S = bank("S")
        counts_ps = S[0:B, 0:NA]
        table_ps = S[0:1, 32:32 + 96]
        rows_ps = S[:, 128:128 + TABU + TILES]
        lora_ps = Hb[:, 0:2 * PAIRS]

        s_cst, s_ident, s_meta = sem("s_cst"), sem("s_ident"), sem("s_meta")
        s_w1, s_bias = sem("s_w1"), sem("s_bias")
        w_in = [sem(f"w_in{k}") for k in range(NW)]
        x_in = [sem(f"x_in{k}") for k in range(4)]
        a_in = [sem(f"a_in{k}") for k in range(2)]
        b_in = [sem(f"b_in{k}") for k in range(2)]
        o_out = [sem(f"o_out{k}") for k in range(4)]
        s_plan = sem("s_plan")
        first_ready = sem("first_ready")
        counts_ready = sem("counts_ready")
        tables_ps_ready = sem("tables_ps_ready")
        table_ready = sem("table_ready")
        lora_rows_ready = sem("lora_rows_ready")
        x_turned, x_hi_ready, x_lo_ready = sem("x_turned"), sem("x_hi_ready"), sem("x_lo_ready")
        w_hi_ready = sem("w_hi_ready")
        w_lo01_ready, w_lo2_ready, w_lo3_ready = sem("w_lo01_ready"), sem("w_lo2_ready"), sem("w_lo3_ready")
        mm_half, mm_done, y_ready, y_turned, x1_ready = sem("mm_half"), sem("mm_done"), sem("y_ready"), sem("y_turned"), sem("x1_ready")
        w1_diag, w1_hi_ready, w1_lo_ready = sem("w1_diag"), sem("w1_hi_ready"), sem("w1_lo_ready")
        x1_hi_ready, x1_lo_ready = sem("x1_hi_ready"), sem("x1_lo_ready")
        a_turned, a_hi_ready, a_lo_ready = sem("a_turned"), sem("a_hi_ready"), sem("a_lo_ready")
        b_hi_ready, b_lo_ready = sem("b_hi_ready"), sem("b_lo_ready")
        h_done, h_own_ready, h_hi_ready, h_lo_ready = sem("h_done"), sem("h_own_ready"), sem("h_hi_ready"), sem("h_lo_ready")
        tile_done, o_free = sem("tile_done"), sem("o_free")
        o_ready = [sem("o_ready0"), sem("o_ready1")]

        row_at = sb("row_at", [P, 4], i32)
        row_copied, row_seen = sem("row_copied"), sem("row_seen")
        block = ctx.enter_context(nc.Block())

        def all_units(eng, unit, after_first=None):
            n = eng.value_load(table[0:1, T_COUNT:T_COUNT + 1], min_val=NA, max_val=MAXU)
            ran = eng.alloc_register(f"ran_{eng.engine.name}")
            last_k = eng.alloc_register(f"last_k_{eng.engine.name}")
            unit(0, 0)
            if after_first:
                after_first()
            unit(1, 1)
            with eng.Fori(2, n, 4) as v:
                unit(v, 2)
                unit(v + 1, 3)
                eng.reg_mov(ran, v + 2)
                eng.reg_mov(last_k, 2)
                with eng.If(v + 2 < n):
                    unit(v + 2, 0)
                    unit(v + 3, 1)
                    eng.reg_mov(ran, v + 4)
                    eng.reg_mov(last_k, 0)
            return eng.snap(ran, min_val=NA, max_val=MAXU), eng.snap(last_k, min_val=0, max_val=2)

        def all_pairs(eng, pair):
            with eng.Fori(0, PAIRS // 2 - 1) as half:
                g = 2 * half
                pair(g, 0, False)
                pair(g + 1, 1, False)
            pair(PAIRS - 2, 0, False)
            pair(PAIRS - 1, 1, True)

        @block.sync
        def _(sp):
            sp.dma_start(mt[:, :], meta).then_inc(s_meta, 16)
            sp.dma_start(cst[:, MASK:NCONST], consts[:, MASK:NCONST]).then_inc(s_ident, 16)
            sp.dma_start(w1_raw[:, :, :], w1).then_inc(s_w1, 16)

            def adapter_in(u, k, column):
                a = sp.value_load(table[0:1, bass.ds(column, 1)], min_val=0, max_val=NA - 1)
                if not isinstance(u, int):
                    sp.wait_ge(w_lo2_ready, u - 2)
                    sp.wait_ge(w_lo3_ready, u - 2)
                sp.dma_start(w_raw[:, k, :, :], weights[bass.ds(a, 1), :, :, :]).then_inc(w_in[k], 16)

            sp.wait_ge(first_ready, 1)
            adapter_in(0, 0, T_FIRST)
            sp.wait_ge(table_ready, 4)
            n = sp.value_load(table[0:1, T_COUNT:T_COUNT + 1], min_val=NA, max_val=MAXU)
            for u in range(1, 4):
                adapter_in(u, u, T_ADAPTER + u)
            with sp.Fori(4, n, 4) as v:
                adapter_in(v, 0, T_ADAPTER + v)
                adapter_in(v + 1, 1, T_ADAPTER + v + 1)
                with sp.If(v + 2 < n):
                    adapter_in(v + 2, 2, T_ADAPTER + v + 2)
                    adapter_in(v + 3, 3, T_ADAPTER + v + 3)
            sp.dma_start(bias_sb[:, :], bias).then_inc(s_bias, 16)

        @block.gpsimd
        def _(pool):
            def gather_x(u, k):
                if not isinstance(u, int) or u >= 4:
                    pool.wait_ge(y_ready, u - 3)
                if isinstance(u, int):
                    at = rows[:, u:u + 1]
                else:
                    pool.tensor_copy(row_at[:, k:k + 1], rows[:, bass.ds(u, 1)]).then_inc(row_copied, 1)
                    pool.wait_ge(row_copied, u - 3)
                    pool.sem_inc(row_seen, 1)
                    at = row_at[:, k:k + 1]
                pool.indirect_dma_start(x_tok[:, k, :], None, x, bass.IndirectOffsetOnAxis(ap=at, axis=0))\
                    .then_inc(x_in[k], 16)

            def gather_lora(g):
                for raw, rows_of, landed in ((a_raw, lora_a, a_in), (b_raw, lora_b, b_in)):
                    pool.indirect_dma_start(raw[:, g % 2, :], None, rows_of,
                                            bass.IndirectOffsetOnAxis(ap=lora_rows[:, g:g + 1], axis=0))\
                        .then_inc(landed[g % 2], 16)

            pool.sem_inc(o_free, 4)
            pool.sem_inc(row_copied, 1)
            pool.wait_ge(s_w1, 16)
            pool.wait_ge(s_ident, 16)
            for c in range(C):
                block_c = w1_raw[:, c, P * c:P * c + P]
                pool.tensor_tensor(block_c, block_c, ident, ALU.add).then_inc(w1_diag, 1)
            pool.wait_ge(table_ready, 1)
            for u in range(3):
                gather_x(u, u)
            pool.wait_ge(table_ready, 4)

            def unit(u, k):
                q = k % 2
                pool.wait_ge(w_hi_ready, 2 * u + 2)
                pool.tensor_tensor(w_lo[:, q, 3, :], w_raw[:, k, 3, :], w_hi[:, q, 3, :], ALU.subtract)\
                    .then_inc(w_lo3_ready, 1)
                gather_x(u + 3, (k + 3) % 4)

            n = pool.value_load(table[0:1, T_COUNT:T_COUNT + 1], min_val=NA, max_val=MAXU)
            unit(0, 0)
            unit(1, 1)
            pool.wait_ge(lora_rows_ready, 1)
            gather_lora(0)
            with pool.Fori(2, n, 4) as v:
                unit(v, 2)
                unit(v + 1, 3)
                with pool.If(v + 2 < n):
                    unit(v + 2, 0)
                    unit(v + 3, 1)

            gather_lora(1)
            for g in range(PAIRS):
                if g + 2 < PAIRS:
                    pool.wait_ge(a_turned, g + 1)
                    pool.wait_ge(b_hi_ready, g + 1)
                    pool.wait_ge(b_lo_ready, g + 1)
                    gather_lora(g + 2)
                for s in range(2):
                    t = 2 * g + s
                    pool.wait_ge(o_ready[s], g + 2)
                    pool.indirect_dma_start(out, bass.IndirectOffsetOnAxis(ap=rows[:, TABU + t:TABU + t + 1], axis=0),
                                            o_tok[:, t % 4, :], None).then_inc(o_out[t % 4], 16)
                    if t >= 2:
                        pool.wait_ge(o_out[(t - 2) % 4], 16 * ((t - 2) // 4 + 1))
                        pool.sem_inc(o_free, 1)
            for k in range(4):
                pool.wait_ge(o_out[k], 16 * TILES // 4)

        @block.scalar
        def _(act):
            act.dma_start(cst[:, 0:MASK], consts[:, 0:MASK]).then_inc(s_cst, 16)
            act.sem_inc(x1_ready, 1)
            act.wait_ge(w1_diag, C)
            act.activation(w1_hi[:, :, :], w1_raw[:, :, :], ACT.Copy).then_inc(w1_hi_ready, 1)

            def take_x1(u, k):
                r = act.value_load(table[0:1, bass.ds(T_RANK + u, 1)], min_val=0, max_val=B)
                act.wait_ge(y_turned, u + 1)
                act.wait_ge(x1_ready, u + 1)
                act.activation(x1T[:, :, bass.ds(T * r, P)], YT[k % 2][:, :].rearrange("p (c t) -> p c t", c=C),
                               ACT.Copy).then_inc(x1_ready, 1)

            def unit(u, k):
                q = k % 2
                act.wait_ge(w_in[k], 4 * (u - k) + 16)
                late = k >= 2 or not isinstance(u, int)
                if late:
                    act.wait_ge(mm_half, u - 1)
                act.activation(w_hi[:, q, 0:2, :], w_raw[:, k, 0:2, :], ACT.Copy).then_inc(w_hi_ready, 1)
                if late:
                    act.wait_ge(mm_done, u - 1)
                act.activation(w_hi[:, q, 2:4, :], w_raw[:, k, 2:4, :], ACT.Copy).then_inc(w_hi_ready, 1)
                act.wait_ge(x_turned, u + 1)
                act.activation(xT_hi[:, q, :], XT[q][:, :], ACT.Copy).then_inc(x_hi_ready, 1)
                if not isinstance(u, int):
                    take_x1(u - 2, k)

            act.wait_ge(table_ready, 4)
            n, _ = all_units(act, unit)

            def round_a(g):
                act.wait_ge(a_turned, g + 1)
                act.wait_ge(h_done, g + 1)
                act.activation(a_hi[:, :], S[:, :], ACT.Copy).then_inc(a_hi_ready, 1)

            def round_b(g, k):
                act.wait_ge(b_in[k], 8 * (g - k) + 16)
                act.wait_ge(tile_done, 2 * g + 1)
                act.activation(b_hi[:, :], b_raw[:, k, :], ACT.Copy).then_inc(b_hi_ready, 1)

            act.wait_ge(x1_ready, n - 1)
            act.activation(x1_hi[:, 0, :, :], x1T[:, :, 0:2 * P], ACT.Copy).then_inc(x1_hi_ready, 1)
            take_x1(n - 2, 0)
            round_b(0, 0)
            round_a(0)
            take_x1(n - 1, 1)
            act.wait_ge(x1_ready, n + 1)

            def pair(g, k, last):
                act.wait_ge(tile_done, 2 * g + 1)
                if not last:
                    act.activation(x1_hi[:, 1 - k, :, :], x1T[:, :, bass.ds(2 * P * (g + 1), 2 * P)], ACT.Copy)\
                        .then_inc(x1_hi_ready, 1)
                act.wait_ge(h_own_ready, g + 1)
                act.activation(h_hi[:, :], h_own[:, :], ACT.Copy).then_inc(h_hi_ready, 1)
                if not last:
                    round_a(g + 1)
                    round_b(g + 1, 1 - k)

            all_pairs(act, pair)

        @block.tensor
        def _(pe):
            pe.sem_inc(tile_done, 1)
            pe.sem_inc(h_done, 1)
            pe.wait_ge(s_cst, 16)
            pe.wait_ge(s_ident, 16)
            pe.wait_ge(s_plan, PLAN_ONEHOT)
            pe.matmul(counts_ps, cst[0:B, ONE:ONE + B], onehot[:, :], start=True, stop=True).then_inc(counts_ready, 1)
            pe.wait_ge(s_plan, PLAN_ALL)
            pe.matmul(table_ps[:, T_ADAPTER:T_ADAPTER + TABU], mf[:, 64:65], place[:, 0:NSLOT:G], start=True, stop=True)
            pe.matmul(table_ps[:, T_RANK:T_RANK + TABU], rank_m[:, :], place[:, 0:NSLOT:G], start=True, stop=True)
            for j in range(G):
                mm = pe.matmul(rows_ps[T * j:T * j + T, :], cst[0:B, B32:B32 + T], place[:, j:NSLOT + B:G],
                               start=True, stop=True)
            mm.then_inc(tables_ps_ready, 1)
            for j in range(G):
                for e in range(2):
                    mm = pe.matmul(lora_ps[T * j:T * j + T, PAIRS * e:PAIRS * (e + 1)], m16[:, :],
                                   place[:, NSLOT + 2 * j + e:NSLOT + B:8], start=True, stop=True)
            mm.then_inc(tables_ps_ready, 1)

            def turn_x(u, k):
                pe.wait_ge(x_in[k], 4 * (u - k) + 16)
                if k >= 2 or not isinstance(u, int):
                    pe.wait_ge(x_lo_ready, u - 1)
                for c in range(C):
                    mm = pe.transpose(XT[k % 2][:, P * c:P * c + P], x_tok[:, k, P * c:P * c + P], ident)
                mm.then_inc(x_turned, 1)

            def turn_y(u, k):
                q = k % 2
                pe.wait_ge(y_ready, u + 1)
                if k >= 2 or not isinstance(u, int):
                    pe.wait_ge(x1_ready, u)
                for c in range(C):
                    mm = pe.transpose(YT[q][:, P * c:P * c + P], y_tok[:, q, P * c:P * c + P], ident)
                mm.then_inc(y_turned, 1)

            def unit(u, k):
                q = k % 2
                for c in range(C):
                    if c == 0:
                        pe.wait_ge(x_lo_ready, u + 1)
                        pe.wait_ge(w_lo01_ready, u + 1)
                    if c == 1:
                        turn_x(u + 1, (k + 1) % 4)
                    if c == 2:
                        if not (isinstance(u, int) and u == 0):
                            turn_y(u - 1, (k - 1) % 4)
                        pe.wait_ge(w_lo2_ready, u + 1)
                    if c == 3:
                        pe.wait_ge(w_lo3_ready, u + 1)
                    xc = slice(P * c, P * c + P)
                    pe.matmul(Y[q][:, :], xT_hi[:, q, xc], w_hi[:, q, c, :], start=(c == 0), stop=False)
                    pe.matmul(Y[q][:, :], xT_hi[:, q, xc], w_lo[:, q, c, :], start=False, stop=False)
                    mm = pe.matmul(Y[q][:, :], xT_lo[:, q, xc], w_hi[:, q, c, :], start=False, stop=(c == C - 1))
                    if c == 1:
                        mm.then_inc(mm_half, 1)
                mm.then_inc(mm_done, 1)

            def turn_a(g, k):
                pe.wait_ge(a_in[k], 8 * (g - k) + 16)
                for c in range(C):
                    mm = pe.transpose(S[:, P * c:P * c + P], a_raw[:, k, P * c:P * c + P], ident)
                mm.then_inc(a_turned, 1)

            turn_x(0, 0)
            n, _ = all_units(pe, unit)
            pe.wait_ge(lora_rows_ready, 1)
            turn_a(0, 0)
            turn_y(n - 1, 1)
            pe.wait_ge(w1_lo_ready, 1)

            def base(s, k, chunks):
                ts = slice(P * s, P * s + P)
                for c in chunks:
                    pe.matmul(Y[s][:, :], x1_hi[:, k, c, ts], w1_hi[:, c, :], start=(c == 0), stop=False)
                    pe.matmul(Y[s][:, :], x1_hi[:, k, c, ts], w1_lo[:, c, :], start=False, stop=False)
                    pe.matmul(Y[s][:, :], x1_lo[:, k, c, ts], w1_hi[:, c, :], start=False, stop=False)

            def adapted(s):
                ts = slice(P * s, P * s + P)
                pe.matmul(Y[s][:, :], h_hi[:, ts], b_hi[:, :], start=False, stop=False)
                pe.matmul(Y[s][:, :], h_hi[:, ts], b_lo[:, :], start=False, stop=False)
                pe.matmul(Y[s][:, :], h_lo[:, ts], b_hi[:, :], start=False, stop=True).then_inc(tile_done, 1)

            def pair(g, k, last):
                pe.wait_ge(x1_lo_ready, g + 1)
                pe.wait_ge(o_ready[0], g + 1)
                base(0, k, range(C))
                pe.wait_ge(a_lo_ready, g + 2)
                for c in range(C):
                    ac = slice(P * c, P * c + P)
                    pe.matmul(Hb[:, 0:2 * P], a_hi[:, ac], x1_hi[:, k, c, :], start=(c == 0), stop=False)
                    pe.matmul(Hb[:, 0:2 * P], a_hi[:, ac], x1_lo[:, k, c, :], start=False, stop=False)
                    mm = pe.matmul(Hb[:, 0:2 * P], a_lo[:, ac], x1_hi[:, k, c, :], start=False, stop=(c == C - 1))
                mm.then_inc(h_done, 1)
                if not last:
                    turn_a(g + 1, 1 - k)
                pe.wait_ge(o_ready[1], g + 1)
                base(1, k, range(C - 1))
                pe.wait_ge(h_lo_ready, g + 2)
                pe.wait_ge(b_lo_ready, g + 1)
                adapted(0)
                base(1, k, range(C - 1, C))
                adapted(1)

            all_pairs(pe, pair)

        @block.vector
        def _(dve):
            steps = [0]

            def step(ins):
                steps[0] += 1
                ins.then_inc(s_plan, 1)

            def settle():
                dve.wait_ge(s_plan, steps[0])

            for credited in (a_lo_ready, h_lo_ready, o_ready[0], o_ready[1]):
                dve.sem_inc(credited, 1)
            iota = cst[0:B, IOTA:IOTA + P]
            dve.wait_ge(s_meta, 16)
            step(dve.tensor_copy(mf[:, :], mt[:, :]))
            settle()
            dve.wait_ge(s_cst, 16)
            step(dve.tensor_scalar(onehot[:, :], iota[:, 0:NA], mf[:, 64:65], None, ALU.is_equal))
            assert steps[0] == PLAN_ONEHOT
            step(dve.tensor_reduce(first[:, :], mf[0:1, 0:B], AX.X, ALU.min))
            step(dve.scalar_tensor_tensor(same[:, :], mf[:, 0:B], mf[:, 64:65], cst[0:B, LT:LT + B],
                                          ALU.is_equal, ALU.mult))
            step(dve.tensor_scalar(below[:, :], iota[:, 0:NA], mf[:, 64:65], None, ALU.is_lt))
            settle()
            dve.tensor_copy(table[:, T_FIRST:T_FIRST + 1], first[:, :]).then_inc(first_ready, 1)
            dve.wait_ge(counts_ready, 1)
            step(dve.tensor_copy(count[:, :], counts_ps))
            settle()
            step(dve.tensor_tensor(fours[:, :, :], count[:, :].unsqueeze(2).to_broadcast([B, NA, NA]),
                                   cst[0:B, K4:K4 + NA].unsqueeze(1).to_broadcast([B, NA, NA]), ALU.is_gt))
            step(dve.tensor_reduce(within[:, :], same[:, :], AX.X, ALU.add))
            step(dve.tensor_tensor(prod[:, 1, :], count[:, :], below[:, :], ALU.mult))
            settle()
            step(dve.tensor_reduce(units_of[:, :], fours[:, :, :], AX.X, ALU.add))
            settle()
            step(dve.tensor_tensor(prod[:, 0, :], units_of[:, :], below[:, :], ALU.mult))
            step(dve.tensor_reduce(n_units[:, :], units_of[:, :], AX.X, ALU.add))
            settle()
            step(dve.tensor_reduce(before[:, :], prod[:, :, :], AX.X, ALU.add))
            step(dve.tensor_copy(table[:, T_COUNT:T_COUNT + 1], n_units[0:1, :]))
            settle()
            step(dve.scalar_tensor_tensor(slot_rank[:, 0:1], before[:, 0:1], float(G), within[:, :], ALU.mult, ALU.add))
            step(dve.tensor_tensor(slot_rank[:, 1:2], before[:, 1:2], within[:, :], ALU.add))
            settle()
            step(dve.tensor_scalar(place[:, 0:NSLOT], iota[:, 0:NSLOT], slot_rank[:, 0:1], None, ALU.is_equal))
            step(dve.tensor_scalar(place[:, NSLOT:NSLOT + B], iota[:, 0:B], slot_rank[:, 1:2], None, ALU.is_equal))
            step(dve.tensor_scalar(rank_m[:, :], slot_rank[:, 1:2], float(-B), None, ALU.add))
            step(dve.tensor_scalar(m16[:, :], cst[0:B, ONE:ONE + 32], mf[:, 65:66], float(R), ALU.mult, ALU.mult))
            assert steps[0] == PLAN_ALL
            dve.wait_ge(tables_ps_ready, 1)
            dve.tensor_scalar(rows[:, :], rows_ps, cst[:, P32:P32 + 1], None, ALU.add).then_inc(table_ready, 1)
            dve.tensor_copy(table[:, T_ADAPTER:T_ADAPTER + TABU], table_ps[:, T_ADAPTER:T_ADAPTER + TABU])\
                .then_inc(table_ready, 1)
            dve.tensor_scalar(table[:, T_RANK:T_RANK + TABU], table_ps[:, T_RANK:T_RANK + TABU], float(B), None,
                              ALU.add).then_inc(table_ready, 2)
            dve.wait_ge(tables_ps_ready, 2)
            dve.tensor_scalar(odd_part[:, :], lora_ps[:, PAIRS:2 * PAIRS], cst[:, ODD:ODD + 1], cst[:, P16:P16 + 1],
                              ALU.mult, ALU.add).then_inc(s_plan, 1)
            dve.tensor_scalar(even_part[:, :], lora_ps[:, 0:PAIRS], cst[:, EVEN:EVEN + 1], None, ALU.mult)\
                .then_inc(s_plan, 1)
            dve.wait_ge(s_plan, PLAN_ALL + 2)
            dve.tensor_tensor(lora_rows[:, :], even_part[:, :], odd_part[:, :], ALU.add).then_inc(lora_rows_ready, 1)
            def add_x(u, q, x_of_u):
                dve.wait_ge(mm_done, u + 1)
                dve.tensor_tensor(y_tok[:, q, :], Y[q][:, :], x_of_u, ALU.add).then_inc(y_ready, 1)

            def unit(u, k):
                q = k % 2
                if not isinstance(u, int):
                    add_x(u - 2, q, x_tok[:, (k - 2) % 4, :])
                dve.wait_ge(w_hi_ready, 2 * u + 1)
                dve.tensor_tensor(w_lo[:, q, 0:2, :], w_raw[:, k, 0:2, :], w_hi[:, q, 0:2, :], ALU.subtract)\
                    .then_inc(w_lo01_ready, 1)
                dve.wait_ge(x_hi_ready, u + 1)
                dve.tensor_tensor(xT_lo[:, q, :], XT[q][:, :], xT_hi[:, q, :], ALU.subtract).then_inc(x_lo_ready, 1)
                dve.wait_ge(w_hi_ready, 2 * u + 2)
                dve.tensor_tensor(w_lo[:, q, 2, :], w_raw[:, k, 2, :], w_hi[:, q, 2, :], ALU.subtract)\
                    .then_inc(w_lo2_ready, 1)

            def split_w1():
                dve.wait_ge(w1_hi_ready, 1)
                dve.tensor_tensor(w1_lo[:, :, :], w1_raw[:, :, :], w1_hi[:, :, :], ALU.subtract).then_inc(w1_lo_ready, 1)

            n, k = all_units(dve, unit, after_first=split_w1)
            x_flat = x_tok[:, :, :].rearrange("p k d -> p (k d)")
            add_x(n - 2, 0, x_flat[:, bass.ds(D * k, D)])
            dve.wait_ge(x1_hi_ready, 1)
            dve.tensor_tensor(x1_lo[:, 0, :, :], x1T[:, :, 0:2 * P], x1_hi[:, 0, :, :], ALU.subtract).then_inc(x1_lo_ready, 1)
            dve.wait_ge(b_hi_ready, 1)
            dve.tensor_tensor(b_lo[:, :], b_raw[:, 0, :], b_hi[:, :], ALU.subtract).then_inc(b_lo_ready, 1)
            add_x(n - 1, 1, x_flat[:, bass.ds(D * (k + 1), D)])
            dve.wait_ge(a_hi_ready, 1)
            dve.tensor_tensor(a_lo[:, :], S[:, :], a_hi[:, :], ALU.subtract).then_inc(a_lo_ready, 1)
            dve.wait_ge(s_bias, 16)

            def pair(g, k, last):
                if not last:
                    dve.wait_ge(x1_hi_ready, g + 2)
                    dve.tensor_tensor(x1_lo[:, 1 - k, :, :], x1T[:, :, bass.ds(2 * P * (g + 1), 2 * P)],
                                      x1_hi[:, 1 - k, :, :], ALU.subtract).then_inc(x1_lo_ready, 1)
                dve.wait_ge(h_done, g + 2)
                dve.wait_ge(h_lo_ready, g + 1)
                dve.tensor_tensor(h_own[:, :], Hb[:, 0:2 * P], cst[:, MASK:MASK + 2 * P], ALU.mult).then_inc(h_own_ready, 1)
                dve.wait_ge(h_hi_ready, g + 1)
                dve.tensor_tensor(h_lo[:, :], h_own[:, :], h_hi[:, :], ALU.subtract).then_inc(h_lo_ready, 1)
                if not last:
                    dve.wait_ge(a_hi_ready, g + 2)
                    dve.tensor_tensor(a_lo[:, :], S[:, :], a_hi[:, :], ALU.subtract).then_inc(a_lo_ready, 1)
                for s in range(2):
                    slot = 2 * k + s
                    dve.wait_ge(tile_done, 2 * g + s + 2)
                    dve.wait_ge(o_free, 2 * g + s + 1)
                    dve.tensor_tensor(o_tok[:, slot, :], Y[s][:, :], bias_sb[:, :], ALU.add).then_inc(o_ready[s], 1)
                if not last:
                    dve.wait_ge(b_hi_ready, g + 2)
                    dve.tensor_tensor(b_lo[:, :], b_raw[:, 1 - k, :], b_hi[:, :], ALU.subtract).then_inc(b_lo_ready, 1)

            all_pairs(dve, pair)


def constants():
    import numpy as np
    p = np.arange(P)
    c = np.zeros((P, NCONST), np.float32)
    b = np.arange(B)
    c[:B, LT:LT + B] = b[None, :] < b[:, None]
    c[:, IOTA:IOTA + P] = p[None, :]
    c[:, K4:K4 + NA] = G * np.arange(NA)
    c[:, B32:B32 + T] = T * p[:, None]
    c[:, P32], c[:, P16] = p % T, p % R
    c[:, ODD], c[:, EVEN] = p // R % 2, 1 - p // R % 2
    c[:, ONE:ONE + B] = 1
    c[:, MASK:MASK + 2 * P] = SCALING * (p[:, None] // R == np.arange(2 * P)[None, :] // T)
    c[:, IDENT:IDENT + P] = np.eye(P)
    return c


def kernel(x, itok_B_0_15, itok_B_0_23, L0_cond_weight, L1_cond_W, L1_cond_b, L1_cond_lora_As, L1_cond_lora_Bs):
    import numpy as np
    import concourse.bacc as bacc
    from concourse.bass_utils import run_bass_kernel_spmd

    ids, ms = np.asarray(itok_B_0_15), np.asarray(itok_B_0_23)
    turned = np.asarray(L0_cond_weight).transpose(0, 2, 1).reshape(NA, C, P, D).transpose(0, 2, 1, 3)
    arrays = {
        "x": np.ascontiguousarray(x).reshape(B * T, D),
        "meta": np.concatenate([np.broadcast_to(ids[None, :], (B, B)), ids[:, None], ms[:, None]], axis=1),
        "weights": turned,
        "w1": np.asarray(L1_cond_W).T.reshape(C, P, D).transpose(1, 0, 2),
        "bias": np.broadcast_to(np.asarray(L1_cond_b)[None, :], (P, D)),
        "lora_a": np.asarray(L1_cond_lora_As).transpose(0, 2, 1).reshape(SLOTS * R, D),
        "lora_b": np.asarray(L1_cond_lora_Bs).reshape(SLOTS * R, D),
        "consts": constants(),
    }
    arrays = {k: np.ascontiguousarray(v) for k, v in arrays.items()}
    nc = bacc.Bacc("TRN2", target_bir_lowering=False, num_devices=1)
    args = [nc.dram_tensor(k, v.shape, mybir.dt.from_np(v.dtype), kind="ExternalInput").ap() for k, v in arrays.items()]
    out = nc.dram_tensor("out", (B * T, D), mybir.dt.float32, kind="ExternalOutput").ap()
    two_adapter_layers(nc, *args, out)
    r = run_bass_kernel_spmd(nc, [arrays], core_ids=[0])
    return r.results[0]["out"].reshape(B, T, D)
```

```python
import concourse.bass as bass
from concourse import mybir
from contextlib import ExitStack

B, T, D = 64, 32, 512
NA, SLOTS, R = 16, 32, 16
SCALING = 2.0
P = 128
C = D // P
G = P // T
MAXU = NA + (B - NA) // G
TABU = MAXU + 3
NSLOT = G * TABU
TILES = B // G
PAIRS = TILES // 2
NW = 4
NLISTS = PAIRS + TILES
HALF = P // 2
RANKS = B + G

IDS, ID, SLOT, LT, IOTA, K4, BROW, ONE = 0, 64, 65, 66, 130, 258, 274, 306
NPLAN = ONE + B
P32, P16, ODD, EVEN, MASK, IDENT = 0, 1, 2, 3, 4, 260
NCONST = IDENT + P
PLAN_ONEHOT, PLAN_ALL = 2, 24
T_VISIT, T_RANK, T_ADAPTER, T_UNITS, T_VISITS, T_FIRST = 0, 32, 64, 88, 89, 90
NV = 20


def two_adapter_layers(nc, x, meta, weights, w1, bias, lora_a, lora_b, consts, out):
    f32, f32r, i32 = mybir.dt.float32, mybir.dt.float32r, mybir.dt.int32
    ALU, ACT, AX = mybir.AluOpType, mybir.ActivationFunctionType, mybir.AxisListType

    ctx = ExitStack()
    with ctx:
        def sb(name, shape, dt=f32):
            return ctx.enter_context(nc.sbuf_tensor(name, shape, dt))

        def bank(name):
            return ctx.enter_context(nc.psum_tensor(name, [P, 512], f32))

        def sem(name):
            return ctx.enter_context(nc.semaphore(name))

        cst = sb("cst", [P, NCONST])
        ident = cst[:, IDENT:IDENT + P]
        mt = sb("mt", [B, NPLAN], i32)
        mf = sb("mf", [B, NPLAN])
        same = sb("same", [B, B])
        within = sb("within", [B, 1])
        onehot = sb("onehot", [B, NA])
        below = sb("below", [B, NA])
        count = sb("count", [B, NA])
        fours = sb("fours", [B, NA, NA])
        units_of = sb("units_of", [B, NA])
        used = sb("used", [B, NA])
        prod = sb("prod", [B, 3, NA])
        before = sb("before", [B, 3])
        of_visit = sb("of_visit", [B, NV])
        leads = sb("leads", [B, 1])
        n_visits = sb("n_visits", [B, 1])
        n_units = sb("n_units", [B, 1])
        first = sb("first", [1, 1])
        slot_rank = sb("slot_rank", [B, 2])
        rank_m = sb("rank_m", [B, 1])
        place = sb("place", [B, NSLOT + B])
        m16 = sb("m16", [B, 32])
        table = sb("table", [1, 96], i32)
        rows = sb("rows", [P, TABU + TILES], i32)
        odd_part = sb("odd_part", [P, NLISTS])
        even_part = sb("even_part", [P, NLISTS])
        lora_rows = sb("lora_rows", [P, NLISTS], i32)

        w_raw = sb("w_raw", [P, NW, C, D])
        w_hi = sb("w_hi", [P, 2, C, D], f32r)
        w_lo = sb("w_lo", [P, 2, C, D], f32r)
        w1_raw = sb("w1_raw", [P, C, D])
        w1_hi = sb("w1_hi", [P, C, D], f32r)
        w1_lo = sb("w1_lo", [P, C, D], f32r)
        x_tok = sb("x_tok", [P, 4, D])
        xT_hi = sb("xT_hi", [P, 2, D], f32r)
        xT_lo = sb("xT_lo", [P, 2, D], f32r)
        y_tok = sb("y_tok", [P, 2, D])
        x1T = sb("x1T", [P, C, RANKS * T])
        x1_hi = sb("x1_hi", [P, 2, C, 2 * P], f32r)
        x1_lo = sb("x1_lo", [P, 2, C, 2 * P], f32r)
        a_raw = sb("a_raw", [P, 2, D])
        b_raw = sb("b_raw", [P, 2, 2, D])
        a_hi = sb("a_hi", [P, D], f32r)
        a_lo = sb("a_lo", [P, D], f32r)
        b_hi = sb("b_hi", [P, 2, D], f32r)
        b_lo = sb("b_lo", [P, 2, D], f32r)
        h_own = sb("h_own", [P, 2 * P])
        h_parts = sb("h_parts", [P, 2 * P], f32r)
        bias_sb = sb("bias_sb", [P, D])
        o_tok = sb("o_tok", [P, 4, D])

        Y = [bank("Y0"), bank("Y1")]
        YT = [bank("YT0"), bank("YT1")]
        XT = [bank("XT0"), bank("XT1")]
        Hb = bank("Hb")
        S = bank("S")
        counts_ps = S[0:B, 0:NA]
        table_ps = S[0:1, 32:32 + 96]
        rows_ps = S[:, 128:128 + TABU + TILES]
        lora_ps = Hb[:, 0:2 * NLISTS]

        s_cst, s_meta = sem("s_cst"), sem("s_meta")
        s_w1, s_bias = sem("s_w1"), sem("s_bias")
        w_in = [sem(f"w_in{k}") for k in range(NW)]
        x_in = [sem(f"x_in{k}") for k in range(4)]
        a_in = [sem(f"a_in{k}") for k in range(2)]
        b_in = [sem(f"b_in{k}") for k in range(2)]
        o_out = [sem(f"o_out{k}") for k in range(4)]
        s_plan = sem("s_plan")
        first_ready = sem("first_ready")
        counts_ready = sem("counts_ready")
        tables_ps_ready = sem("tables_ps_ready")
        table_ready = sem("table_ready")
        lora_rows_ready = sem("lora_rows_ready")
        x_turned, x_hi_ready, x_lo_ready = sem("x_turned"), sem("x_hi_ready"), sem("x_lo_ready")
        w_here = sem("w_here")
        w_hi01_ready, w_hi23_ready = sem("w_hi01_ready"), sem("w_hi23_ready")
        w_lo01_ready, w_lo23_ready = sem("w_lo01_ready"), sem("w_lo23_ready")
        mm_half, mm_done, y_ready, y_turned, x1_ready = sem("mm_half"), sem("mm_done"), sem("y_ready"), sem("y_turned"), sem("x1_ready")
        w1_diag, w1_hi_ready, w1_lo_ready = sem("w1_diag"), sem("w1_hi_ready"), sem("w1_lo_ready")
        x1_hi_ready, x1_lo_ready = sem("x1_hi_ready"), sem("x1_lo_ready")
        a_turned, a_hi_ready, a_lo_ready = sem("a_turned"), sem("a_hi_ready"), sem("a_lo_ready")
        b_hi_ready, b_lo_ready = sem("b_hi_ready"), sem("b_lo_ready")
        h_done, h_own_ready, h_hi_ready, h_lo_ready = sem("h_done"), sem("h_own_ready"), sem("h_hi_ready"), sem("h_lo_ready")
        tile_done, o_free = sem("tile_done"), sem("o_free")
        o_ready = [sem("o_ready0"), sem("o_ready1")]

        row_at = sb("row_at", [P, 4], i32)
        row_copied, row_seen = sem("row_copied"), sem("row_seen")
        block = ctx.enter_context(nc.Block())

        def all_units(eng, unit, after_first=None):
            n = eng.value_load(table[0:1, T_UNITS:T_UNITS + 1], min_val=NA, max_val=MAXU)
            ran = eng.alloc_register(f"ran_{eng.engine.name}")
            last_k = eng.alloc_register(f"last_k_{eng.engine.name}")
            unit(0, 0)
            if after_first:
                after_first()
            unit(1, 1)
            with eng.Fori(2, n, 4) as v:
                unit(v, 2)
                unit(v + 1, 3)
                eng.reg_mov(ran, v + 2)
                eng.reg_mov(last_k, 2)
                with eng.If(v + 2 < n):
                    unit(v + 2, 0)
                    unit(v + 3, 1)
                    eng.reg_mov(ran, v + 4)
                    eng.reg_mov(last_k, 0)
            return eng.snap(ran, min_val=NA, max_val=MAXU), eng.snap(last_k, min_val=0, max_val=2)

        raw_flat = w_raw[:, :, :, :].rearrange("p n c d -> p (n c d)")
        hi_flat = w_hi[:, :, :, :].rearrange("p n c d -> p (n c d)")
        lo_flat = w_lo[:, :, :, :].rearrange("p n c d -> p (n c d)")

        class Visit:
            def __init__(self, eng):
                self.eng = eng
                self.seen, self.step, self.raw, self.half = [
                    eng.alloc_register(f"{what}_{eng.engine.name}") for what in ("seen", "step", "raw", "half")]

            def first(self):
                self.eng.reg_mov(self.seen, 1)

            def look_at(self, u):
                eng = self.eng
                before_u = eng.snap(self.seen, min_val=1, max_val=NA)
                seen = eng.value_load(table[0:1, bass.ds(T_VISIT + u, 1)], min_val=1, max_val=NA)
                eng.reg_mov(self.step, seen - before_u)
                eng.reg_mov(self.raw, C * D * ((seen + (NW - 1)) & (NW - 1)))
                eng.reg_mov(self.half, C * D * ((seen + 1) & 1))
                eng.reg_mov(self.seen, seen)

            def if_new(self, split):
                eng = self.eng
                with eng.If(eng.snap(self.step, min_val=-NA, max_val=NA) > 0):
                    split(eng.snap(self.seen, min_val=1, max_val=NA),
                          eng.snap(self.raw, min_val=0, max_val=C * D * (NW - 1)),
                          eng.snap(self.half, min_val=0, max_val=C * D))

        def all_pairs(eng, pair):
            with eng.Fori(0, PAIRS // 2 - 1) as half:
                g = 2 * half
                pair(g, 0, False)
                pair(g + 1, 1, False)
            pair(PAIRS - 2, 0, False)
            pair(PAIRS - 1, 1, True)

        @block.sync
        def _(sp):
            sp.dma_start(mt[:, :], meta).then_inc(s_meta, 16)
            sp.dma_start(cst[:, :], consts).then_inc(s_cst, 16)
            sp.dma_start(w1_raw[:, :, :], w1).then_inc(s_w1, 16)

            def adapter_in(j, k, column):
                a = sp.value_load(table[0:1, bass.ds(column, 1)], min_val=0, max_val=NA - 1)
                if not isinstance(j, int):
                    sp.wait_ge(w_lo01_ready, j - 3)
                    sp.wait_ge(w_lo23_ready, j - 3)
                sp.dma_start(w_raw[:, k, :, :], weights[bass.ds(a, 1), :, :, :]).then_inc(w_in[k], 16)

            def report(j, k):
                sp.wait_ge(w_in[k], 4 * (j - k) + 16)
                sp.sem_inc(w_here, 1)

            sp.wait_ge(first_ready, 1)
            adapter_in(0, 0, T_FIRST)
            sp.wait_ge(table_ready, 6)
            n = sp.value_load(table[0:1, T_VISITS:T_VISITS + 1], min_val=1, max_val=NA)
            for j in range(1, NW):
                adapter_in(j, j, T_ADAPTER + j)
                report(j - 1, j - 1)
            issued1, issued3 = sp.alloc_register("issued1"), sp.alloc_register("issued3")
            sp.reg_mov(issued1, 16)
            sp.reg_mov(issued3, 16)
            with sp.If(n > NW):
                with sp.Fori(4, n, 4) as v:
                    adapter_in(v, 0, T_ADAPTER + v)
                    report(v - 1, 3)
                    adapter_in(v + 1, 1, T_ADAPTER + v + 1)
                    report(v, 0)
                    sp.reg_mov(issued1, 4 * v + 16)
                    with sp.If(v + 2 < n):
                        adapter_in(v + 2, 2, T_ADAPTER + v + 2)
                        report(v + 1, 1)
                        adapter_in(v + 3, 3, T_ADAPTER + v + 3)
                        report(v + 2, 2)
                        sp.reg_mov(issued3, 4 * v + 16)
            all1, all3 = sp.snap(issued1), sp.snap(issued3)
            sp.wait_ge(w_in[1], all1)
            sp.wait_ge(w_in[3], all3)
            sp.sem_inc(w_here, 1)
            sp.dma_start(bias_sb[:, :], bias).then_inc(s_bias, 16)

        @block.gpsimd
        def _(pool):
            def gather_x(u, k):
                if not isinstance(u, int) or u >= 4:
                    pool.wait_ge(y_ready, u - 3)
                if isinstance(u, int):
                    at = rows[:, u:u + 1]
                else:
                    pool.tensor_copy(row_at[:, k:k + 1], rows[:, bass.ds(u, 1)]).then_inc(row_copied, 1)
                    pool.wait_ge(row_copied, u - 3)
                    pool.sem_inc(row_seen, 1)
                    at = row_at[:, k:k + 1]
                pool.indirect_dma_start(x_tok[:, k, :], None, x, bass.IndirectOffsetOnAxis(ap=at, axis=0))\
                    .then_inc(x_in[k], 16)

            def gather_lora(g):
                for part in range(3):
                    gather_lora_part(g, part)

            def gather_lora_part(g, part):
                gathers = [(a_raw[:, g % 2, :], lora_a, g, a_in)] + [
                    (b_raw[:, g % 2, s, :], lora_b, PAIRS + 2 * g + s, b_in) for s in range(2)]
                raw, rows_of, column, landed = gathers[part]
                pool.indirect_dma_start(raw, None, rows_of,
                                        bass.IndirectOffsetOnAxis(ap=lora_rows[:, column:column + 1], axis=0))\
                    .then_inc(landed[g % 2], 16)

            pool.sem_inc(o_free, 4)
            pool.sem_inc(row_copied, 1)
            pool.wait_ge(s_w1, 16)
            pool.wait_ge(s_cst, 16)
            for c in range(C):
                block_c = w1_raw[:, c, P * c:P * c + P]
                pool.tensor_tensor(block_c, block_c, ident, ALU.add).then_inc(w1_diag, 1)
            pool.wait_ge(table_ready, 1)
            for u in range(3):
                gather_x(u, u)
            pool.wait_ge(table_ready, 6)

            visit = Visit(pool)
            visit.first()

            def split(seen, raw, half):
                pool.wait_ge(w_hi23_ready, seen)
                pool.tensor_tensor(lo_flat[:, bass.ds(half + 2 * D, 2 * D)], raw_flat[:, bass.ds(raw + 2 * D, 2 * D)],
                                   hi_flat[:, bass.ds(half + 2 * D, 2 * D)], ALU.subtract).then_inc(w_lo23_ready, 1)

            def unit(u, k):
                if isinstance(u, int) and u == 0:
                    split(1, 0, 0)
                else:
                    visit.if_new(split)
                visit.look_at(u + 1)
                gather_x(u + 3, (k + 3) % 4)

            n = pool.value_load(table[0:1, T_UNITS:T_UNITS + 1], min_val=NA, max_val=MAXU)
            unit(0, 0)
            unit(1, 1)
            pool.wait_ge(lora_rows_ready, 1)
            for part in range(3):
                with pool.Fori(2 + 4 * part, 6 + 4 * part, 4) as v:
                    unit(v, 2)
                    unit(v + 1, 3)
                    unit(v + 2, 0)
                    unit(v + 3, 1)
                gather_lora_part(0, part)
            with pool.Fori(14, n, 4) as v:
                unit(v, 2)
                unit(v + 1, 3)
                with pool.If(v + 2 < n):
                    unit(v + 2, 0)
                    unit(v + 3, 1)

            gather_lora(1)
            for g in range(PAIRS):
                if g + 2 < PAIRS:
                    pool.wait_ge(a_turned, g + 1)
                    pool.wait_ge(b_hi_ready, g + 1)
                    pool.wait_ge(b_lo_ready, g + 1)
                    gather_lora(g + 2)
                for s in range(2):
                    t = 2 * g + s
                    pool.wait_ge(o_ready[s], g + 2)
                    pool.indirect_dma_start(out, bass.IndirectOffsetOnAxis(ap=rows[:, TABU + t:TABU + t + 1], axis=0),
                                            o_tok[:, t % 4, :], None).then_inc(o_out[t % 4], 16)
                    if t >= 2:
                        pool.wait_ge(o_out[(t - 2) % 4], 16 * ((t - 2) // 4 + 1))
                        pool.sem_inc(o_free, 1)
            for k in range(4):
                pool.wait_ge(o_out[k], 16 * TILES // 4)

        @block.scalar
        def _(act):
            act.sem_inc(x1_ready, 1)
            act.wait_ge(w1_diag, C)
            act.activation(w1_hi[:, :, :], w1_raw[:, :, :], ACT.Copy).then_inc(w1_hi_ready, 1)

            def rank_of(u):
                return act.value_load(table[0:1, bass.ds(T_RANK + u, 1)], min_val=0, max_val=B)

            def take_x1(u, k, r):
                act.wait_ge(y_turned, u + 1)
                act.wait_ge(x1_ready, u + 1)
                act.activation(x1T[:, :, bass.ds(T * r, P)], YT[k % 2][:, :].rearrange("p (c t) -> p c t", c=C),
                               ACT.Copy).then_inc(x1_ready, 1)

            visit = Visit(act)
            visit.first()

            def unit(u, k):
                q = k % 2
                late = k >= 2 or not isinstance(u, int)

                def split(seen, raw, half):
                    act.wait_ge(w_here, seen)
                    if late:
                        act.wait_ge(mm_half, u - 1)
                    act.activation(hi_flat[:, bass.ds(half, 2 * D)], raw_flat[:, bass.ds(raw, 2 * D)], ACT.Copy)\
                        .then_inc(w_hi01_ready, 1)
                    if late:
                        act.wait_ge(mm_done, u - 1)
                    act.activation(hi_flat[:, bass.ds(half + 2 * D, 2 * D)], raw_flat[:, bass.ds(raw + 2 * D, 2 * D)],
                                   ACT.Copy).then_inc(w_hi23_ready, 1)

                if isinstance(u, int) and u == 0:
                    split(1, 0, 0)
                else:
                    visit.if_new(split)
                if not isinstance(u, int):
                    r = rank_of(u - 2)
                if late:
                    act.wait_ge(mm_done, u - 1)
                act.wait_ge(x_turned, u + 1)
                act.activation(xT_hi[:, q, :], XT[q][:, :], ACT.Copy).then_inc(x_hi_ready, 1)
                visit.look_at(u + 1)
                if not isinstance(u, int):
                    take_x1(u - 2, k, r)

            act.wait_ge(table_ready, 6)
            n, _ = all_units(act, unit)

            def round_a(g):
                act.wait_ge(a_turned, g + 1)
                act.wait_ge(h_done, g + 1)
                act.activation(a_hi[:, :], S[:, :], ACT.Copy).then_inc(a_hi_ready, 1)

            def round_b(g, k):
                act.wait_ge(b_in[k], 16 * (g - k) + 32)
                act.wait_ge(tile_done, 2 * g + 1)
                act.activation(b_hi[:, :, :], b_raw[:, k, :, :], ACT.Copy).then_inc(b_hi_ready, 1)

            act.wait_ge(x1_ready, n - 1)
            act.activation(x1_hi[:, 0, :, :], x1T[:, :, 0:2 * P], ACT.Copy).then_inc(x1_hi_ready, 1)
            take_x1(n - 2, 0, rank_of(n - 2))
            round_b(0, 0)
            round_a(0)
            take_x1(n - 1, 1, rank_of(n - 1))
            act.wait_ge(x1_ready, n + 1)

            def pair(g, k, last):
                act.wait_ge(tile_done, 2 * g + 1)
                if not last:
                    act.activation(x1_hi[:, 1 - k, :, :], x1T[:, :, bass.ds(2 * P * (g + 1), 2 * P)], ACT.Copy)\
                        .then_inc(x1_hi_ready, 1)
                act.wait_ge(h_own_ready, g + 1)
                for s in range(2):
                    ts, own = slice(P * s, P * s + P), slice(HALF * s, HALF * s + HALF)
                    act.activation(h_parts[own, ts], h_own[own, ts], ACT.Copy).then_inc(h_hi_ready, 1)
                if not last:
                    round_a(g + 1)
                    round_b(g + 1, 1 - k)

            all_pairs(act, pair)

        @block.tensor
        def _(pe):
            pe.sem_inc(tile_done, 1)
            pe.sem_inc(h_done, 1)
            pe.wait_ge(s_plan, PLAN_ONEHOT)
            pe.matmul(counts_ps, mf[:, ONE:ONE + B], onehot[:, :], start=True, stop=True).then_inc(counts_ready, 1)
            pe.wait_ge(s_plan, PLAN_ALL)
            pe.matmul(table_ps[:, T_VISIT:T_VISIT + TABU], before[:, 2:3], place[:, 0:NSLOT:G], start=True, stop=True)
            pe.matmul(table_ps[:, T_ADAPTER:T_ADAPTER + NV], mf[:, ID:ID + 1], of_visit[:, :], start=True, stop=True)
            pe.matmul(table_ps[:, T_RANK:T_RANK + TABU], rank_m[:, :], place[:, 0:NSLOT:G], start=True, stop=True)
            for j in range(G):
                mm = pe.matmul(rows_ps[T * j:T * j + T, :], mf[:, BROW:BROW + T], place[:, j:NSLOT + B:G],
                               start=True, stop=True)
            mm.then_inc(tables_ps_ready, 1)
            for j in range(G):
                for e in range(2):
                    quarter = lora_ps[T * j:T * j + T, NLISTS * e:NLISTS * (e + 1)]
                    pe.matmul(quarter[:, 0:PAIRS], m16[:, :], place[:, NSLOT + 2 * j + e:NSLOT + B:8], start=True, stop=True)
                    mm = pe.matmul(quarter[:, PAIRS:NLISTS], m16[:, :], place[:, NSLOT + 2 * (j % 2) + e:NSLOT + B:G],
                                   start=True, stop=True)
            mm.then_inc(tables_ps_ready, 1)

            def turn_x(u, k):
                pe.wait_ge(x_in[k], 4 * (u - k) + 16)
                if k >= 2 or not isinstance(u, int):
                    pe.wait_ge(x_lo_ready, u - 1)
                for c in range(C):
                    mm = pe.transpose(XT[k % 2][:, P * c:P * c + P], x_tok[:, k, P * c:P * c + P], ident)
                mm.then_inc(x_turned, 1)

            def turn_y(u, k):
                q = k % 2
                pe.wait_ge(y_ready, u + 1)
                if k >= 2 or not isinstance(u, int):
                    pe.wait_ge(x1_ready, u)
                for c in range(C):
                    mm = pe.transpose(YT[q][:, P * c:P * c + P], y_tok[:, q, P * c:P * c + P], ident)
                mm.then_inc(y_turned, 1)

            seen_pe = pe.alloc_register("seen_pe")

            def products(u, k, seen, half):
                q = k % 2
                for c in range(C):
                    if c == 0:
                        pe.wait_ge(w_lo01_ready, seen)
                        pe.wait_ge(x_lo_ready, u + 1)
                    if c == 1:
                        turn_x(u + 1, (k + 1) % 4)
                    if c == 2:
                        if not (isinstance(u, int) and u == 0):
                            turn_y(u - 1, (k - 1) % 4)
                        pe.wait_ge(w_lo23_ready, seen)
                    if c == 3:
                        next_seen = pe.value_load(table[0:1, bass.ds(T_VISIT + u + 1, 1)], min_val=1, max_val=NA)
                        pe.reg_mov(seen_pe, next_seen)
                    xc = slice(P * c, P * c + P)
                    pe.matmul(Y[q][:, :], xT_hi[:, q, xc], w_hi[:, half, c, :], start=(c == 0), stop=False)
                    pe.matmul(Y[q][:, :], xT_hi[:, q, xc], w_lo[:, half, c, :], start=False, stop=False)
                    mm = pe.matmul(Y[q][:, :], xT_lo[:, q, xc], w_hi[:, half, c, :], start=False, stop=(c == C - 1))
                    if c == 1:
                        mm.then_inc(mm_half, 1)
                mm.then_inc(mm_done, 1)

            def unit(u, k):
                if isinstance(u, int) and u == 0:
                    products(u, k, 1, 0)
                    return
                seen = pe.snap(seen_pe, min_val=1, max_val=NA)
                with pe.If((seen & 1) > 0):
                    products(u, k, seen, 0)
                with pe.Else():
                    products(u, k, seen, 1)

            def turn_a(g, k):
                pe.wait_ge(a_in[k], 8 * (g - k) + 16)
                for c in range(C):
                    mm = pe.transpose(S[:, P * c:P * c + P], a_raw[:, k, P * c:P * c + P], ident)
                mm.then_inc(a_turned, 1)

            def keep_warm(times):
                for _ in range(times):
                    pe.matmul(XT[1][:, 0:2 * P], ident, cst[:, MASK:MASK + 2 * P], start=True, stop=True)

            pe.wait_ge(s_cst, 16)
            keep_warm(3)
            turn_x(0, 0)
            keep_warm(2)
            pe.wait_ge(table_ready, 6)
            n, _ = all_units(pe, unit)
            pe.wait_ge(lora_rows_ready, 1)
            turn_a(0, 0)
            turn_y(n - 1, 1)
            pe.wait_ge(w1_lo_ready, 1)

            def base(s, k, chunks):
                ts = slice(P * s, P * s + P)
                for c in chunks:
                    pe.matmul(Y[s][:, :], x1_hi[:, k, c, ts], w1_hi[:, c, :], start=(c == 0), stop=False)
                    pe.matmul(Y[s][:, :], x1_hi[:, k, c, ts], w1_lo[:, c, :], start=False, stop=False)
                    pe.matmul(Y[s][:, :], x1_lo[:, k, c, ts], w1_hi[:, c, :], start=False, stop=False)

            def adapted(s):
                ts = slice(P * s, P * s + P)
                pe.matmul(Y[s][:, :], h_parts[:, ts], b_hi[:, s, :], start=False, stop=False)
                pe.matmul(Y[s][:, :], h_parts[:, ts], b_lo[:, s, :], start=False, stop=True).then_inc(tile_done, 1)

            def pair(g, k, last):
                pe.wait_ge(x1_lo_ready, g + 1)
                pe.wait_ge(o_ready[0], g + 1)
                base(0, k, range(C))
                pe.wait_ge(a_lo_ready, g + 2)
                for c in range(C):
                    ac = slice(P * c, P * c + P)
                    pe.matmul(Hb[:, 0:2 * P], a_hi[:, ac], x1_hi[:, k, c, :], start=(c == 0), stop=False)
                    pe.matmul(Hb[:, 0:2 * P], a_hi[:, ac], x1_lo[:, k, c, :], start=False, stop=False)
                    mm = pe.matmul(Hb[:, 0:2 * P], a_lo[:, ac], x1_hi[:, k, c, :], start=False, stop=(c == C - 1))
                mm.then_inc(h_done, 1)
                if not last:
                    turn_a(g + 1, 1 - k)
                pe.wait_ge(o_ready[1], g + 1)
                base(1, k, range(C - 1))
                pe.wait_ge(h_lo_ready, g + 2)
                pe.wait_ge(b_lo_ready, g + 1)
                adapted(0)
                base(1, k, range(C - 1, C))
                adapted(1)

            all_pairs(pe, pair)

        @block.vector
        def _(dve):
            steps = [0]

            def step(ins):
                steps[0] += 1
                ins.then_inc(s_plan, 1)

            def settle():
                dve.wait_ge(s_plan, steps[0])

            for credited in (a_lo_ready, h_lo_ready, o_ready[0], o_ready[1]):
                dve.sem_inc(credited, 1)
            iota = mf[:, IOTA:IOTA + P]
            dve.wait_ge(s_meta, 16)
            step(dve.tensor_copy(mf[:, :], mt[:, :]))
            settle()
            step(dve.tensor_scalar(onehot[:, :], iota[:, 0:NA], mf[:, ID:ID + 1], None, ALU.is_equal))
            assert steps[0] == PLAN_ONEHOT
            step(dve.tensor_reduce(first[:, :], mf[0:1, 0:B], AX.X, ALU.min))
            step(dve.scalar_tensor_tensor(same[:, :], mf[:, 0:B], mf[:, ID:ID + 1], mf[:, LT:LT + B],
                                          ALU.is_equal, ALU.mult))
            step(dve.tensor_scalar(below[:, :], iota[:, 0:NA], mf[:, ID:ID + 1], None, ALU.is_lt))
            settle()
            dve.tensor_copy(table[:, T_FIRST:T_FIRST + 1], first[:, :]).then_inc(first_ready, 1)
            dve.wait_ge(counts_ready, 1)
            step(dve.tensor_copy(count[:, :], counts_ps))
            settle()
            step(dve.tensor_tensor(fours[:, :, :], count[:, :].unsqueeze(2).to_broadcast([B, NA, NA]),
                                   mf[:, K4:K4 + NA].unsqueeze(1).to_broadcast([B, NA, NA]), ALU.is_gt))
            step(dve.tensor_reduce(within[:, :], same[:, :], AX.X, ALU.add))
            step(dve.tensor_tensor(prod[:, 1, :], count[:, :], below[:, :], ALU.mult))
            step(dve.tensor_scalar(used[:, :], count[:, :], 0.0, None, ALU.is_gt))
            settle()
            step(dve.tensor_reduce(units_of[:, :], fours[:, :, :], AX.X, ALU.add))
            settle()
            step(dve.tensor_tensor(prod[:, 0, :], units_of[:, :], below[:, :], ALU.mult))
            step(dve.tensor_tensor(prod[:, 2, :], used[:, :], below[:, :], ALU.mult))
            step(dve.tensor_reduce(n_visits[:, :], used[:, :], AX.X, ALU.add))
            step(dve.tensor_reduce(n_units[:, :], units_of[:, :], AX.X, ALU.add))
            settle()
            step(dve.tensor_reduce(before[:, :], prod[:, :, :], AX.X, ALU.add))
            step(dve.tensor_scalar(leads[:, :], within[:, :], 0.0, None, ALU.is_equal))
            settle()
            step(dve.scalar_tensor_tensor(slot_rank[:, 0:1], before[:, 0:1], float(G), within[:, :], ALU.mult, ALU.add))
            step(dve.tensor_tensor(slot_rank[:, 1:2], before[:, 1:2], within[:, :], ALU.add))
            settle()
            step(dve.tensor_scalar(place[:, 0:NSLOT], iota[:, 0:NSLOT], slot_rank[:, 0:1], None, ALU.is_equal))
            step(dve.tensor_scalar(place[:, NSLOT:NSLOT + B], iota[:, 0:B], slot_rank[:, 1:2], None, ALU.is_equal))
            step(dve.tensor_scalar(rank_m[:, :], slot_rank[:, 1:2], float(-B), None, ALU.add))
            step(dve.tensor_scalar(of_visit[:, :], iota[:, 0:NV], before[:, 2:3], leads[:, :], ALU.is_equal, ALU.mult))
            step(dve.tensor_scalar(m16[:, :], mf[:, ONE:ONE + 32], mf[:, SLOT:SLOT + 1], float(R), ALU.mult, ALU.mult))
            assert steps[0] == PLAN_ALL
            dve.wait_ge(s_cst, 16)
            dve.wait_ge(tables_ps_ready, 1)
            dve.tensor_scalar(rows[:, :], rows_ps, cst[:, P32:P32 + 1], None, ALU.add).then_inc(table_ready, 1)
            dve.tensor_copy(table[:, T_ADAPTER:T_ADAPTER + NV], table_ps[:, T_ADAPTER:T_ADAPTER + NV]).then_inc(table_ready, 1)
            dve.tensor_scalar(table[:, T_VISIT:T_VISIT + TABU], table_ps[:, T_VISIT:T_VISIT + TABU], 1.0, None,
                              ALU.add).then_inc(table_ready, 1)
            dve.tensor_copy(table[:, T_UNITS:T_UNITS + 1], n_units[0:1, :]).then_inc(table_ready, 1)
            dve.tensor_copy(table[:, T_VISITS:T_VISITS + 1], n_visits[0:1, :]).then_inc(table_ready, 1)
            dve.tensor_scalar(table[:, T_RANK:T_RANK + TABU], table_ps[:, T_RANK:T_RANK + TABU], float(B), None,
                              ALU.add).then_inc(table_ready, 1)
            dve.wait_ge(tables_ps_ready, 2)
            dve.tensor_scalar(odd_part[:, :], lora_ps[:, NLISTS:2 * NLISTS], cst[:, ODD:ODD + 1], cst[:, P16:P16 + 1],
                              ALU.mult, ALU.add).then_inc(s_plan, 1)
            dve.tensor_scalar(even_part[:, :], lora_ps[:, 0:NLISTS], cst[:, EVEN:EVEN + 1], None, ALU.mult)\
                .then_inc(s_plan, 1)
            dve.wait_ge(s_plan, PLAN_ALL + 2)
            dve.tensor_tensor(lora_rows[:, :], even_part[:, :], odd_part[:, :], ALU.add).then_inc(lora_rows_ready, 1)
            def add_x(u, q, x_of_u):
                dve.wait_ge(mm_done, u + 1)
                dve.tensor_tensor(y_tok[:, q, :], Y[q][:, :], x_of_u, ALU.add).then_inc(y_ready, 1)

            visit = Visit(dve)
            visit.first()

            def split(seen, raw, half):
                dve.wait_ge(w_hi01_ready, seen)
                dve.tensor_tensor(lo_flat[:, bass.ds(half, 2 * D)], raw_flat[:, bass.ds(raw, 2 * D)],
                                  hi_flat[:, bass.ds(half, 2 * D)], ALU.subtract).then_inc(w_lo01_ready, 1)

            def unit(u, k):
                q = k % 2
                if not isinstance(u, int):
                    add_x(u - 2, q, x_tok[:, (k - 2) % 4, :])
                if isinstance(u, int) and u == 0:
                    split(1, 0, 0)
                else:
                    visit.if_new(split)
                visit.look_at(u + 1)
                dve.wait_ge(x_hi_ready, u + 1)
                dve.tensor_tensor(xT_lo[:, q, :], XT[q][:, :], xT_hi[:, q, :], ALU.subtract).then_inc(x_lo_ready, 1)

            def split_w1():
                dve.wait_ge(w1_hi_ready, 1)
                dve.tensor_tensor(w1_lo[:, :, :], w1_raw[:, :, :], w1_hi[:, :, :], ALU.subtract).then_inc(w1_lo_ready, 1)

            n, k = all_units(dve, unit, after_first=split_w1)
            x_flat = x_tok[:, :, :].rearrange("p k d -> p (k d)")
            add_x(n - 2, 0, x_flat[:, bass.ds(D * k, D)])
            dve.wait_ge(x1_hi_ready, 1)
            dve.tensor_tensor(x1_lo[:, 0, :, :], x1T[:, :, 0:2 * P], x1_hi[:, 0, :, :], ALU.subtract).then_inc(x1_lo_ready, 1)
            add_x(n - 1, 1, x_flat[:, bass.ds(D * (k + 1), D)])
            dve.wait_ge(a_hi_ready, 1)
            dve.tensor_tensor(a_lo[:, :], S[:, :], a_hi[:, :], ALU.subtract).then_inc(a_lo_ready, 1)
            dve.wait_ge(b_hi_ready, 1)
            dve.tensor_tensor(b_lo[:, :, :], b_raw[:, 0, :, :], b_hi[:, :, :], ALU.subtract).then_inc(b_lo_ready, 1)
            dve.wait_ge(s_bias, 16)

            def pair(g, k, last):
                if not last:
                    dve.wait_ge(x1_hi_ready, g + 2)
                    dve.tensor_tensor(x1_lo[:, 1 - k, :, :], x1T[:, :, bass.ds(2 * P * (g + 1), 2 * P)],
                                      x1_hi[:, 1 - k, :, :], ALU.subtract).then_inc(x1_lo_ready, 1)
                dve.wait_ge(h_done, g + 2)
                dve.wait_ge(h_lo_ready, g + 1)
                dve.tensor_tensor(h_own[:, :], Hb[:, 0:2 * P], cst[:, MASK:MASK + 2 * P], ALU.mult).then_inc(h_own_ready, 1)
                for s in range(2):
                    ts, own = slice(P * s, P * s + P), slice(HALF * s, HALF * s + HALF)
                    free = slice(HALF * (1 - s), HALF * (2 - s))
                    dve.wait_ge(h_hi_ready, 2 * g + s + 1)
                    ins = dve.tensor_tensor(h_parts[free, ts], h_own[own, ts], h_parts[own, ts], ALU.subtract)
                ins.then_inc(h_lo_ready, 1)
                if not last:
                    dve.wait_ge(a_hi_ready, g + 2)
                    dve.tensor_tensor(a_lo[:, :], S[:, :], a_hi[:, :], ALU.subtract).then_inc(a_lo_ready, 1)
                for s in range(2):
                    slot = 2 * k + s
                    dve.wait_ge(tile_done, 2 * g + s + 2)
                    dve.wait_ge(o_free, 2 * g + s + 1)
                    dve.tensor_tensor(o_tok[:, slot, :], Y[s][:, :], bias_sb[:, :], ALU.add).then_inc(o_ready[s], 1)
                if not last:
                    dve.wait_ge(b_hi_ready, g + 2)
                    dve.tensor_tensor(b_lo[:, :, :], b_raw[:, 1 - k, :, :], b_hi[:, :, :], ALU.subtract).then_inc(b_lo_ready, 1)

            all_pairs(dve, pair)


def integers(ids, slots):
    import numpy as np
    b = np.arange(B)
    c = np.zeros((B, NPLAN), ids.dtype)
    c[:, IDS:IDS + B], c[:, ID], c[:, SLOT] = ids[None, :], ids, slots
    c[:, LT:LT + B] = b[None, :] < b[:, None]
    c[:, IOTA:IOTA + P] = np.arange(P)[None, :]
    c[:, K4:K4 + NA] = G * np.arange(NA)
    c[:, BROW:BROW + T] = T * b[:, None]
    c[:, ONE:ONE + B] = 1
    return c


def constants():
    import numpy as np
    p = np.arange(P)
    c = np.zeros((P, NCONST), np.float32)
    c[:, P32], c[:, P16] = p % T, p % R
    c[:, ODD], c[:, EVEN] = p // R % 2, 1 - p // R % 2
    c[:, MASK:MASK + 2 * P] = SCALING * (p[:, None] // R == np.arange(2 * P)[None, :] // T)
    c[:, IDENT:IDENT + P] = np.eye(P)
    return c


def kernel(x, itok_B_0_15, itok_B_0_23, L0_cond_weight, L1_cond_W, L1_cond_b, L1_cond_lora_As, L1_cond_lora_Bs):
    import numpy as np
    import concourse.bacc as bacc
    from concourse.bass_utils import run_bass_kernel_spmd

    ids, ms = np.asarray(itok_B_0_15), np.asarray(itok_B_0_23)
    turned = np.asarray(L0_cond_weight).transpose(0, 2, 1).reshape(NA, C, P, D).transpose(0, 2, 1, 3)
    arrays = {
        "x": np.ascontiguousarray(x).reshape(B * T, D),
        "meta": integers(ids, ms),
        "weights": turned,
        "w1": np.asarray(L1_cond_W).T.reshape(C, P, D).transpose(1, 0, 2),
        "bias": np.broadcast_to(np.asarray(L1_cond_b)[None, :], (P, D)),
        "lora_a": np.asarray(L1_cond_lora_As).transpose(0, 2, 1).reshape(SLOTS * R, D),
        "lora_b": np.asarray(L1_cond_lora_Bs).reshape(SLOTS * R, D),
        "consts": constants(),
    }
    arrays = {k: np.ascontiguousarray(v) for k, v in arrays.items()}
    nc = bacc.Bacc("TRN2", target_bir_lowering=False, num_devices=1)
    args = [nc.dram_tensor(k, v.shape, mybir.dt.from_np(v.dtype), kind="ExternalInput").ap() for k, v in arrays.items()]
    out = nc.dram_tensor("out", (B * T, D), mybir.dt.float32, kind="ExternalOutput").ap()
    two_adapter_layers(nc, *args, out)
    r = run_bass_kernel_spmd(nc, [arrays], core_ids=[0])
    return r.results[0]["out"].reshape(B, T, D)
```
